# Optimizing a Trainium2 kernel written in Bass

```python
import numpy as np
import jax
import jax.numpy as jnp

def _softmax(x, axis=-1):
    return jax.nn.softmax(x, axis=axis)

def _gelu(x):
    return jax.nn.gelu(x, approximate=True)

def _silu(x):
    return jax.nn.silu(x)

def _sigmoid(x):
    return jax.nn.sigmoid(x)

def _layernorm(x, axis=-1, eps=1e-05):
    m = jnp.mean(x, axis=axis, keepdims=True)
    v = jnp.var(x, axis=axis, keepdims=True)
    return (x - m) / jnp.sqrt(v + eps)

def _scatter_add(tgt, idx, src, axis=0):
    return tgt.at[idx].add(src)

def _segment_sum(src, seg, n):
    return jax.ops.segment_sum(src, seg, n)
kernel_name = 'mk_conv_attn_hybrid_d2_conv_nchw1024_r4_f72ebf'

def setup_inputs(seed: int=0):
    np.random.seed(seed)
    _w = jnp.asarray

    def _rec_inputs():
        import jax
        import jax.numpy as jnp
        _gk = jax.random.key(seed)
        x = -7.109e-06 + 0.09999 * jax.random.normal(jax.random.fold_in(_gk, 1), (16, 256, 16, 16), jnp.float32)
        return x
    x = _rec_inputs()

    def _L0_conv_setup():
        import jax, jax.numpy as jnp
        import numpy as np
        B, N, Fh, T, K, C = (16, 256, 16, 16, 3, 16)

        def _col_softmax(S):
            return jax.nn.softmax(S, axis=1)
        key = jax.random.key(seed)
        ks = jax.random.split(key, 16)
        rn = lambda k, shape, s: jax.random.normal(k, shape, dtype=jnp.float32) * s
        x = rn(ks[0], (B, N, Fh, T), 0.1)
        cheb = rn(ks[1], (K, N, N), 1.0 / np.sqrt(N))
        Theta = rn(ks[2], (K, Fh, C), (2.0 / (Fh + C)) ** 0.5)
        W1 = rn(ks[3], (T,), T ** (-0.5))
        W2 = rn(ks[4], (Fh, T), (2.0 / (Fh + T)) ** 0.5)
        W3 = rn(ks[5], (Fh,), Fh ** (-0.5))
        b_s = jnp.zeros((1, N, N), jnp.float32)
        V_s = rn(ks[6], (N, N), N ** (-0.5))
        U1 = rn(ks[7], (N,), N ** (-0.5))
        U2 = rn(ks[8], (Fh, N), (2.0 / (Fh + N)) ** 0.5)
        U3 = rn(ks[9], (Fh,), Fh ** (-0.5))
        b_e = jnp.zeros((1, T, T), jnp.float32)
        V_e = rn(ks[10], (T, T), T ** (-0.5))
        tw = rn(ks[11], (C, C, 1, 3), (2.0 / (C * 3)) ** 0.5)
        tb = jnp.zeros((C,), jnp.float32)
        rw = rn(ks[12], (C, Fh), (2.0 / Fh) ** 0.5)
        rb = jnp.zeros((C,), jnp.float32)
        gamma = jnp.ones((C,), jnp.float32)
        beta = jnp.zeros((C,), jnp.float32)
        return dict(x=x, cheb=cheb, Theta=Theta, W1=W1, W2=W2, W3=W3, b_s=b_s, V_s=V_s, U1=U1, U2=U2, U3=U3, b_e=b_e, V_e=V_e, tw=tw, tb=tb, rw=rw, rb=rb, gamma=gamma, beta=beta)
    _L0_conv_all = _L0_conv_setup()
    _L0_conv_in = {k: v for k, v in _L0_conv_all.items() if k in ('cheb', 'Theta', 'W1', 'W2', 'W3', 'b_s', 'V_s', 'U1', 'U2', 'U3', 'b_e', 'V_e', 'tw', 'tb', 'rw', 'rb', 'gamma', 'beta')}
    del _L0_conv_all

    def _L1_attn_setup():
        import jax, jax.numpy as jnp
        import numpy as np
        EPS = 1e-05
        NUM_HEADS = 16

        def _linear_attention(x, Wq, Wk, Wv, Wo, bo):
            B, L, E = x.shape
            H = NUM_HEADS
            D = E // H
            q = (x @ Wq.T).reshape(B, L, H, D)
            k = (x @ Wk.T).reshape(B, L, H, D)
            v = (x @ Wv.T).reshape(B, L, H, D)
            phi_q = jax.nn.elu(q) + 1.0
            phi_k = jax.nn.elu(k) + 1.0
            pq = jnp.moveaxis(phi_q, 1, 0)
            pk = jnp.moveaxis(phi_k, 1, 0)
            vt = jnp.moveaxis(v, 1, 0)
            S0 = jnp.zeros((B, H, D, D), x.dtype)
            z0 = jnp.zeros((B, H, D), x.dtype)

            def step(carry, inp):
                S, z = carry
                pq_t, pk_t, v_t = inp
                S = S + pk_t[..., :, None] * v_t[..., None, :]
                z = z + pk_t
                num = jnp.einsum('bhd,bhde->bhe', pq_t, S)
                den = jnp.sum(pq_t * z, axis=-1, keepdims=True) + EPS
                return ((S, z), num / den)
            (_, _), out = jax.lax.scan(step, (S0, z0), (pq, pk, vt))
            out = jnp.moveaxis(out, 0, 1).reshape(B, L, E)
            return out @ Wo.T + bo
        key = jax.random.key(seed)
        ks = jax.random.split(key, 6)
        B, L, E = (4, 1024, 256)
        s = 1.0 / np.sqrt(E)
        return {'x': jax.random.normal(ks[0], (B, L, E), jnp.float32), 'Wq': jax.random.normal(ks[1], (E, E), jnp.float32) * s, 'Wk': jax.random.normal(ks[2], (E, E), jnp.float32) * s, 'Wv': jax.random.normal(ks[3], (E, E), jnp.float32) * s, 'Wo': jax.random.normal(ks[4], (E, E), jnp.float32) * s, 'bo': jnp.zeros((E,), jnp.float32)}
    _L1_attn_all = _L1_attn_setup()
    _L1_attn_in = {k: v for k, v in _L1_attn_all.items() if k in ('Wq', 'Wk', 'Wv', 'Wo', 'bo')}
    del _L1_attn_all

    def _L1_ffn_setup():
        import jax, jax.numpy as jnp
        import numpy as np
        E = 16
        G = 4
        EPG = E // G
        K = 4
        TOPK_GROUP = 2
        PER_GROUP_K = K // TOPK_GROUP

        def _route(xf, router_w, correction_bias):
            S = xf.shape[0]
            logits = xf @ router_w.T
            scores = jax.nn.sigmoid(logits)
            sb = scores + correction_bias
            grp_top = jax.lax.top_k(sb.reshape(S, G, EPG), PER_GROUP_K)[0]
            group_scores = grp_top.sum(axis=-1)
            _, group_idx = jax.lax.top_k(group_scores, TOPK_GROUP)
            group_mask = jnp.zeros((S, G), sb.dtype).at[jnp.arange(S)[:, None], group_idx].set(1.0)
            score_mask = jnp.broadcast_to(group_mask[:, :, None], (S, G, EPG)).reshape(S, E)
            masked = jnp.where(score_mask > 0, sb, -jnp.inf)
            _, topk_idx = jax.lax.top_k(masked, K)
            w = jnp.take_along_axis(scores, topk_idx, axis=1)
            w = w / (w.sum(axis=-1, keepdims=True) + 1e-20)
            return (topk_idx, w, scores)
        key = jax.random.key(seed)
        ks = jax.random.split(key, 9)
        B, T, C, H, HS = (2, 256, 256, 64, 512)
        std = 0.02
        return {'x': jax.random.normal(ks[0], (B, T, C), jnp.float32), 'router_w': jax.random.normal(ks[1], (E, C), jnp.float32) * std, 'correction_bias': jnp.zeros((E,), jnp.float32), 'gate_w': jax.random.normal(ks[2], (E, C, H), jnp.float32) * std, 'up_w': jax.random.normal(ks[3], (E, C, H), jnp.float32) * std, 'down_w': jax.random.normal(ks[4], (E, H, C), jnp.float32) * std, 'shared_gate_w': jax.random.normal(ks[5], (HS, C), jnp.float32) * std, 'shared_up_w': jax.random.normal(ks[6], (HS, C), jnp.float32) * std, 'shared_down_w': jax.random.normal(ks[7], (C, HS), jnp.float32) * std}
    _L1_ffn_all = _L1_ffn_setup()
    _L1_ffn_in = {k: v for k, v in _L1_ffn_all.items() if k in ('router_w', 'correction_bias', 'gate_w', 'up_w', 'down_w', 'shared_gate_w', 'shared_up_w', 'shared_down_w')}
    del _L1_ffn_all
    return {'x': x, 'L0_conv_cheb': _L0_conv_in['cheb'], 'L0_conv_Theta': _L0_conv_in['Theta'], 'L0_conv_W1': _L0_conv_in['W1'], 'L0_conv_W2': _L0_conv_in['W2'], 'L0_conv_W3': _L0_conv_in['W3'], 'L0_conv_b_s': _L0_conv_in['b_s'], 'L0_conv_V_s': _L0_conv_in['V_s'], 'L0_conv_U1': _L0_conv_in['U1'], 'L0_conv_U2': _L0_conv_in['U2'], 'L0_conv_U3': _L0_conv_in['U3'], 'L0_conv_b_e': _L0_conv_in['b_e'], 'L0_conv_V_e': _L0_conv_in['V_e'], 'L0_conv_tw': _L0_conv_in['tw'], 'L0_conv_tb': _L0_conv_in['tb'], 'L0_conv_rw': _L0_conv_in['rw'], 'L0_conv_rb': _L0_conv_in['rb'], 'L0_conv_gamma': _L0_conv_in['gamma'], 'L0_conv_beta': _L0_conv_in['beta'], 'L1_attn_Wq': _L1_attn_in['Wq'], 'L1_attn_Wk': _L1_attn_in['Wk'], 'L1_attn_Wv': _L1_attn_in['Wv'], 'L1_attn_Wo': _L1_attn_in['Wo'], 'L1_attn_bo': _L1_attn_in['bo'], 'L1_ffn_router_w': _L1_ffn_in['router_w'], 'L1_ffn_correction_bias': _L1_ffn_in['correction_bias'], 'L1_ffn_gate_w': _L1_ffn_in['gate_w'], 'L1_ffn_up_w': _L1_ffn_in['up_w'], 'L1_ffn_down_w': _L1_ffn_in['down_w'], 'L1_ffn_shared_gate_w': _L1_ffn_in['shared_gate_w'], 'L1_ffn_shared_up_w': _L1_ffn_in['shared_up_w'], 'L1_ffn_shared_down_w': _L1_ffn_in['shared_down_w']}

def reference(x, L0_conv_cheb, L0_conv_Theta, L0_conv_W1, L0_conv_W2, L0_conv_W3, L0_conv_b_s, L0_conv_V_s, L0_conv_U1, L0_conv_U2, L0_conv_U3, L0_conv_b_e, L0_conv_V_e, L0_conv_tw, L0_conv_tb, L0_conv_rw, L0_conv_rb, L0_conv_gamma, L0_conv_beta, L1_attn_Wq, L1_attn_Wk, L1_attn_Wv, L1_attn_Wo, L1_attn_bo, L1_ffn_router_w, L1_ffn_correction_bias, L1_ffn_gate_w, L1_ffn_up_w, L1_ffn_down_w, L1_ffn_shared_gate_w, L1_ffn_shared_up_w, L1_ffn_shared_down_w):
    import jax
    import jax.numpy as jnp

    def _L0_conv_ref(x, cheb, Theta, W1, W2, W3, b_s, V_s, U1, U2, U3, b_e, V_e, tw, tb, rw, rb, gamma, beta):
        import jax, jax.numpy as jnp
        import numpy as np
        B, N, Fh, T, K, C = (16, 256, 16, 16, 3, 16)

        def _col_softmax(S):
            return jax.nn.softmax(S, axis=1)
        lhs = jnp.einsum('bnft,n->btf', x, U1) @ U2
        rhs = jnp.einsum('f,bnft->bnt', U3, x)
        prod = jnp.einsum('btn,bns->bts', lhs, rhs)
        E = jnp.einsum('kj,bij->bik', V_e, jax.nn.sigmoid(prod + b_e))
        E = _col_softmax(E)
        x_tat = jnp.einsum('bnfj,bjt->bnft', x, E)
        lhs2 = jnp.einsum('bnft,t->bnf', x_tat, W1) @ W2
        rhs2 = jnp.einsum('f,bnft->btn', W3, x_tat)
        prod2 = jnp.einsum('bnt,btm->bnm', lhs2, rhs2)
        S = jnp.einsum('kj,bij->bik', V_s, jax.nn.sigmoid(prod2 + b_s))
        S = _col_softmax(S)
        out = jnp.zeros((B, N, C, T), x.dtype)
        for k in range(cheb.shape[0]):
            r = jnp.einsum('mn,bmn,bmft->bnft', cheb[k], S, x)
            out = out + jnp.einsum('bnft,fo->bnot', r, Theta[k])
        sg = jax.nn.relu(out)
        tc = jax.lax.conv_general_dilated(sg.transpose(0, 2, 1, 3), tw, (1, 1), ((0, 0), (1, 1)), dimension_numbers=('NCHW', 'OIHW', 'NCHW'))
        tc = (tc + tb[None, :, None, None]).transpose(0, 2, 1, 3)
        res = jnp.einsum('bnft,of->bnot', x, rw) + rb[None, None, :, None]
        y = jax.nn.relu(res + tc)
        mu = jnp.mean(y, axis=-1, keepdims=True)
        var = jnp.var(y, axis=-1, keepdims=True)
        return (y - mu) / jnp.sqrt(var + 1e-05) * gamma + beta

    def _L1_attn_ref(x, Wq, Wk, Wv, Wo, bo):
        import jax, jax.numpy as jnp
        import numpy as np
        EPS = 1e-05
        NUM_HEADS = 16

        def _linear_attention(x, Wq, Wk, Wv, Wo, bo):
            B, L, E = x.shape
            H = NUM_HEADS
            D = E // H
            q = (x @ Wq.T).reshape(B, L, H, D)
            k = (x @ Wk.T).reshape(B, L, H, D)
            v = (x @ Wv.T).reshape(B, L, H, D)
            phi_q = jax.nn.elu(q) + 1.0
            phi_k = jax.nn.elu(k) + 1.0
            pq = jnp.moveaxis(phi_q, 1, 0)
            pk = jnp.moveaxis(phi_k, 1, 0)
            vt = jnp.moveaxis(v, 1, 0)
            S0 = jnp.zeros((B, H, D, D), x.dtype)
            z0 = jnp.zeros((B, H, D), x.dtype)

            def step(carry, inp):
                S, z = carry
                pq_t, pk_t, v_t = inp
                S = S + pk_t[..., :, None] * v_t[..., None, :]
                z = z + pk_t
                num = jnp.einsum('bhd,bhde->bhe', pq_t, S)
                den = jnp.sum(pq_t * z, axis=-1, keepdims=True) + EPS
                return ((S, z), num / den)
            (_, _), out = jax.lax.scan(step, (S0, z0), (pq, pk, vt))
            out = jnp.moveaxis(out, 0, 1).reshape(B, L, E)
            return out @ Wo.T + bo
        return _linear_attention(x, Wq, Wk, Wv, Wo, bo)

    def _L1_ffn_ref(x, router_w, correction_bias, gate_w, up_w, down_w, shared_gate_w, shared_up_w, shared_down_w):
        import jax, jax.numpy as jnp
        import numpy as np
        E = 16
        G = 4
        EPG = E // G
        K = 4
        TOPK_GROUP = 2
        PER_GROUP_K = K // TOPK_GROUP

        def _route(xf, router_w, correction_bias):
            S = xf.shape[0]
            logits = xf @ router_w.T
            scores = jax.nn.sigmoid(logits)
            sb = scores + correction_bias
            grp_top = jax.lax.top_k(sb.reshape(S, G, EPG), PER_GROUP_K)[0]
            group_scores = grp_top.sum(axis=-1)
            _, group_idx = jax.lax.top_k(group_scores, TOPK_GROUP)
            group_mask = jnp.zeros((S, G), sb.dtype).at[jnp.arange(S)[:, None], group_idx].set(1.0)
            score_mask = jnp.broadcast_to(group_mask[:, :, None], (S, G, EPG)).reshape(S, E)
            masked = jnp.where(score_mask > 0, sb, -jnp.inf)
            _, topk_idx = jax.lax.top_k(masked, K)
            w = jnp.take_along_axis(scores, topk_idx, axis=1)
            w = w / (w.sum(axis=-1, keepdims=True) + 1e-20)
            return (topk_idx, w, scores)
        B, T, C = x.shape
        S = B * T
        xf = x.reshape(S, C)
        sg = xf @ shared_gate_w.T
        su = xf @ shared_up_w.T
        shared_out = jax.nn.silu(sg) * su @ shared_down_w.T
        topk_idx, w, _scores = _route(xf, router_w, correction_bias)
        combine = jnp.zeros((S, E), xf.dtype).at[jnp.arange(S)[:, None], topk_idx].add(w)
        g = jnp.einsum('sc,ech->esh', xf, gate_w)
        u = jnp.einsum('sc,ech->esh', xf, up_w)
        h = jax.nn.silu(g) * u
        hw = h * combine.T[:, :, None]
        routed = jnp.einsum('esh,ehc->sc', hw, down_w)
        return (shared_out + routed).reshape(B, T, C)

    def _gn(v, G=32, eps=1e-05):
        B_, C_, H_, W_ = v.shape
        g = v.reshape(B_, G, C_ // G, H_, W_)
        m = jnp.mean(g, axis=(2, 3, 4), keepdims=True)
        s = jnp.var(g, axis=(2, 3, 4), keepdims=True)
        return ((g - m) / jnp.sqrt(s + eps)).reshape(v.shape)

    def _ln_c(v, eps=1e-06):
        m = jnp.mean(v, axis=1, keepdims=True)
        s = jnp.var(v, axis=1, keepdims=True)
        return (v - m) / jnp.sqrt(s + eps)

    def _ln_t(v, eps=1e-05):
        m = jnp.mean(v, axis=-1, keepdims=True)
        s = jnp.var(v, axis=-1, keepdims=True)
        return (v - m) / jnp.sqrt(s + eps)

    def _to_tokens(v):
        B_, C_, H_, W_ = v.shape
        return v.reshape(B_, C_, H_ * W_).transpose(0, 2, 1)

    def _from_tokens(t, like):
        B_, C_, H_, W_ = like.shape
        return t.transpose(0, 2, 1).reshape(B_, C_, H_, W_)
    x = x + _L0_conv_ref(_gn(x), L0_conv_cheb, L0_conv_Theta, L0_conv_W1, L0_conv_W2, L0_conv_W3, L0_conv_b_s, L0_conv_V_s, L0_conv_U1, L0_conv_U2, L0_conv_U3, L0_conv_b_e, L0_conv_V_e, L0_conv_tw, L0_conv_tb, L0_conv_rw, L0_conv_rb, L0_conv_gamma, L0_conv_beta)
    t = _to_tokens(x)
    t = t + _L1_attn_ref(_ln_t(t), L1_attn_Wq, L1_attn_Wk, L1_attn_Wv, L1_attn_Wo, L1_attn_bo)
    t = t + _L1_ffn_ref(_ln_t(t), L1_ffn_router_w, L1_ffn_correction_bias, L1_ffn_gate_w, L1_ffn_up_w, L1_ffn_down_w, L1_ffn_shared_gate_w, L1_ffn_shared_up_w, L1_ffn_shared_down_w)
    x = _from_tokens(t, x)
    return x

_drawn_inputs = setup_inputs


def setup_inputs(seed=0):
    import zlib

    import numpy as np

    out = dict(_drawn_inputs(seed))
    spreads = {'L0_conv_b_s': (0.0, 0.8),
     'L0_conv_b_e': (0.0, 0.8),
     'L0_conv_tb': (0.0, 0.295),
     'L0_conv_rb': (0.0, 0.429),
     'L0_conv_gamma': (1.0, 0.2),
     'L0_conv_beta': (0.0, 0.8),
     'L1_attn_bo': (0.0, 0.1),
     'L1_ffn_correction_bias': (0.0, 0.8)}
    factors = {'L0_conv_cheb': 8.0,
     'L0_conv_Theta': 8.0,
     'L0_conv_W1': 8.0,
     'L0_conv_W2': 8.0,
     'L0_conv_W3': 8.0,
     'L0_conv_V_s': 8.0,
     'L0_conv_U1': 8.0,
     'L0_conv_U2': 8.0,
     'L0_conv_U3': 8.0,
     'L0_conv_V_e': 8.0,
     'L0_conv_tw': 8.0,
     'L1_attn_Wq': 3.251,
     'L1_ffn_router_w': 8.0,
     'L1_ffn_gate_w': 8.0,
     'L1_ffn_up_w': 8.0,
     'L1_ffn_down_w': 8.0,
     'L1_ffn_shared_gate_w': 7.771,
     'L1_ffn_shared_up_w': 7.619,
     'L1_ffn_shared_down_w': 7.676}
    for name, (base, spread) in spreads.items():
        noise = np.random.default_rng([zlib.crc32(name.encode()), seed]).standard_normal(out[name].shape)
        drawn = base * np.exp(spread * noise) if base else spread * noise
        out[name] = jnp.asarray(drawn.astype(out[name].dtype))
    for name, factor in factors.items():
        out[name] = (out[name] * factor).astype(out[name].dtype)
    return out
```

```python
import concourse.bass as bass
from concourse import mybir
from contextlib import ExitStack

F32 = mybir.dt.float32
F32R = mybir.dt.float32r
ALU = mybir.AluOpType
ACT = mybir.ActivationFunctionType
AX = mybir.AxisListType

P = 128
B = 16
N = 256
T = 16
L = 256
PAIRS = B // 2
HEADS = 16
EXPERTS = 16
HIDDEN = 64
SHARED = 512
FF = EXPERTS * HIDDEN + SHARED
CHUNKS = FF // P
ROUTED = EXPERTS * HIDDEN // P
BIG = 3e30
UNCHOSEN = -1e30
FILLER = -2e30

SMALL = {}
CONST = {}


def columns(table, parts):
    at = 0
    for name, width in parts:
        table[name] = (at, at + width)
        at += width
    return at


N_SMALL = columns(SMALL, [("u1", 256), ("u2", 256), ("u3", 1), ("w3", 1), ("w2", 16), ("w1", 1), ("ve", 16),
                          ("be", 16), ("tb", 16), ("rb", 16), ("gamma", 16), ("beta", 16), ("bo", 2),
                          ("router", 32), ("corr", 16)])
N_CONST = columns(CONST, [("ident", 128), ("mean8", 128), ("heads16", 128), ("causal", 128), ("even", 1), ("odd", 1),
                          ("halves", 32), ("head", 8), ("diag8", 8)])


class Signal:

    def __init__(self, sem, names, start=0):
        self.sem, self.names, self.start = sem, names, start
        self.turn = 0

    def at(self, pair, name):
        return pair * len(self.names) + self.names.index(name) + 1 + self.start

    def mark(self, name):
        assert self.names[self.turn % len(self.names)] == name, (name, self.names[self.turn % len(self.names)])
        self.turn += 1
        return self.sem, 1


FRONT = [("gn", 3), ("xT0", 1), ("xT1", 1), ("R", .5), ("y000", 0), ("M", .5), ("y001", 0), ("prod", 1), ("y010", 0),
         ("Epre", 2.5), ("y011", 0), ("Erep", 1.5), ("y100", 0), ("lr", 1.5), ("y101", 0), ("p2_0", 0), ("p2_1", 1),
         ("y110", 0), ("sp0", 0), ("y111", .5), ("sp1", 1.5), ("st0", 1), ("st1", 1), ("o0", 0), ("o1", 0.5), ("tc0", 0), ("tc1", 12),
         ("tok0", 1), ("tok1", 3), ("xl0", 0), ("xl1", 1), ("k0", 0), ("k1", 0), ("q0", 0), ("q1", 0), ("v0", 0), ("v1", 1),
         ("kt", 0.5), ("kv", 0), ("dent", 1), ("rd0", 0), ("rd1", 0), ("P0", 1), ("P1", 1.5), ("wo0", 0), ("wo1", 1),
         ("tk0", 1), ("tk1", 3), ("xn0", 0), ("xn1", 0), ("lg", 1.5), ("rt", 4), ("cb", 0)]
FRONT_NAMES = [name for name, _ in FRONT]


def ffn_steps():
    steps = []
    for j in range(CHUNKS):
        steps.append(("gu", j))
        if j < ROUTED:
            steps.append(("cm", j))
        if j:
            steps.append(("dn", j - 1))
    return steps + [("dn", CHUNKS - 1), ("out", 0)]


def schedule():
    ffn = ffn_steps()
    total = sum(w for _, w in FRONT)
    out, used, placed = [], 0.0, 0
    barrier = FRONT_NAMES.index("xn0")
    last_gu = ffn.index(("gu", CHUNKS - 1)) + 1
    for i, (name, weight) in enumerate(FRONT):
        if i == barrier:
            while placed < last_gu:
                out.append(ffn[placed])
                placed += 1
        out.append(("front", name))
        used += weight
        while placed < min(len(ffn), round(used / total * len(ffn))):
            out.append(ffn[placed])
            placed += 1
    out += ffn[placed:]
    return out


SCORES = [f"s{b}{lc}{j}" for b in range(2) for lc in range(2) for j in range(4)]
TILES = [n for n in FRONT_NAMES[:FRONT_NAMES.index("P0")]] + SCORES + FRONT_NAMES[FRONT_NAMES.index("P1") + 1:]
RING = 3
SLOTS = -(-len(TILES) // RING) * RING


def graph_attention_moe(nc, x, out, small, consts, spread_rows, cheb, theta, tconv, vsT, bsT, wqkvT, woT, gateT, upT, down):
    x_v = x.rearrange("(p b) (c n) f t -> p b n c (f t)", b=2, n=P)
    out_v = out.rearrange("(p b) (c n) f t -> p b n c (f t)", b=2, n=P)
    with ExitStack() as ctx:
        def sb(name, shape, dt=F32):
            return ctx.enter_context(nc.sbuf_tensor(name, shape, dt))

        def sem(name):
            return ctx.enter_context(nc.semaphore(name))

        sm = sb("small_parameters", [P, N_SMALL])
        cs = sb("constants", [P, N_CONST])
        cheb_s = sb("cheb_s", [P, 3, 2, N])
        theta_s = sb("theta_s", [P, 4, 8, T])
        tconv_s = sb("tconv_s", [P, 10, T])
        vs_s = sb("vs_s", [P, 2, N])
        bs_s = sb("bs_s", [P, 2, N])
        u3blk = sb("u3blk", [P, 8])
        ve_h = sb("ve_h", [T, 4, T])
        carrier = sb("carrier", [1, 2])
        iw1 = sb("iw1", [T, 18])
        biasy = sb("biasy", [P, T])
        wqkv_h = sb("wqkv_h", [P, 2, 768], F32R)
        wqkv_l = sb("wqkv_l", [P, 2, 768], F32R)
        wo_s = sb("wo_s", [P, 2, N])
        router_h = sb("router_h", [P, 2, P], F32R)
        router_l = sb("router_l", [P, 2, P], F32R)
        gate_h = sb("gate_h", [P, 2, FF], F32R)
        gate_l = sb("gate_l", [P, 2, FF], F32R)
        up_h = sb("up_h", [P, 2, FF], F32R)
        up_l = sb("up_l", [P, 2, FF], F32R)
        down_h = sb("down_h", [P, CHUNKS, N], F32R)
        down_l = sb("down_l", [P, CHUNKS, N], F32R)
        spread = sb("spread", [32, ROUTED, P], F32R)
        scratch = sb("scratch", [P, 3072])
        x2k = scratch[:, 0:1024].rearrange("p (c n) -> p c n", c=2)
        y_out = scratch[:, 1024:2048].rearrange("p (c n) -> p c n", c=2)
        sl = scratch[:, 2048:2560]
        hb = scratch[:, 2560:3072]

        def small_at(name, rows=P):
            a, b = SMALL[name]
            return sm[0:rows, a:b]

        def const_at(name, rows=P):
            a, b = CONST[name]
            return cs[0:rows, a:b]

        ident = const_at("ident")

        x_s = sb("x_s", [P, 2, 2, L])
        stats = sb("stats", [P, 4, 6])
        mv = sb("mv", [P, 4, 2])
        gmv = sb("gmv", [P, 4, 2])
        gsq = sb("gsq", [P, 4])
        gvar = sb("gvar", [P, 4])
        grstd = sb("grstd", [P, 4])
        lsum = sb("lsum", [P, 2, 2])
        lm = sb("lm", [P, 2, 2, T])
        r_s = sb("r_s", [P, 2, 2, T])
        m_s = sb("m_s", [P, 2 * T])
        te = sb("te", [T, 2, T])
        emax = sb("emax", [T, 2])
        esum = sb("esum", [T, 2])
        eT = sb("eT", [T, 2, T])
        ab = sb("ab", [P, 4, 64])
        shared = sb("shared", [P, 9728])
        place = [0]

        def part(*shape):
            size = 1
            for s in shape:
                size *= s
            a = place[0]
            place[0] += size
            v = shared[:, a:a + size]
            names = "abcd"[:len(shape)]
            if len(shape) == 1:
                return v
            return v.rearrange(f"p ({' '.join(names)}) -> p {' '.join(names)}", **{n: s for n, s in zip(names, shape)})

        xg = part(2, 2, L)
        sT = part(2, 2, N)
        xT = part(2, 2, N)
        th = part(2, 2, N)
        place[0] -= 2048
        a_1 = part(3, 2, N)
        place[0] += 512
        a_s = [part(3, 2, N), a_1]
        y_s = part(2, 2, 2, 384)
        resb = part(2, 2, 256)
        sg, z, zsq = xg, th, sT
        junk = a_s[0][:, 0, 0, :]
        eTx = a_s[0][0:T, 0].rearrange("p c n -> p (c n)").rearrange("p (b j f) -> p b j f", b=2, j=T)
        l2 = a_s[0][0:T, 1].rearrange("p c n -> p (c n)")
        r2 = a_s[0][0:T, 2].rearrange("p c n -> p (c n)")
        conv_end = place[0]
        place[0] = 0
        xt = part(2, 2, N)
        e_s = part(2, 512)
        k_f = part(2, 512)
        q_f = part(2, 512)
        q_e = part(2, 512)
        q_o = part(2, 512)
        ktok = part(512)
        kvm = part(512)
        zs = part(2, 512)
        rd_s = xt.rearrange("p b c n -> p b (c n)")
        attn = e_s
        rdx = zs.rearrange("p c n -> p (c n)").rearrange("p (q h e) -> p q h e", q=4, h=HEADS)
        p_s = part(3, 512)
        assert max(place[0], conv_end) <= 9728, (place[0], conv_end)

        smax = sb("smax", [P, 2, 2])
        ssum = sb("ssum", [P, 2, 2])
        rinv = sb("rinv", [P, 2, 2])
        msum = sb("msum", [P, 2, 32])
        vsum = sb("vsum", [P, 2, 32])
        vrstd = sb("vrstd", [P, 2, 32])
        x1 = sb("x1", [P, 2, 2, L])
        tst = sb("tst", [P, 4, 6])
        tmv = sb("tmv", [P, 4, 2])
        tve = sb("tve", [P, 4])
        trs = sb("trs", [P, 4])
        xa_h = sb("xa_h", [P, 2, 512], F32R)
        xa_l = sb("xa_l", [P, 2, 512], F32R)
        v_s = sb("v_s", [P, 2, 2, 8, 48])
        minus_half = sb("minus_half", [P, 32])
        one = sb("one", [P, 1])
        rd = sb("rd", [P, 4, HEADS])
        x2 = x1[:, :, :, :].rearrange("p c b l -> p c (b l)")
        xf_h = sb("xf_h", [P, 2, 512], F32R)
        xf_l = sb("xf_l", [P, 2, 512], F32R)
        lgT = k_f[0:EXPERTS, 0, :]
        sc = sb("sc", [P, 4, EXPERTS])
        scb = sb("scb", [P, 4, EXPERTS])
        pairs = sb("pairs", [P, 16, 6])
        gs = sb("gs", [P, 4, 10])
        gtop = sb("gtop", [P, 4, 8])
        gtake = sb("gtake", [P, 4, 8])
        gmark = sb("gmark", [P, 4, 10])
        gneg = sb("gneg", [P, 4, 4])
        es = sb("es", [P, 4, 20])
        etop = sb("etop", [P, 4, 8])
        etake = sb("etake", [P, 4, 8])
        emark = sb("emark", [P, 4, 20])
        wsel = sb("wsel", [P, 4, EXPERTS])
        wsum = sb("wsum", [P, 4])
        whl = sb("whl", [P, 4, 2, EXPERTS], F32R)
        comb = sb("comb", [32, 512], F32R)
        hh = sb("hh", [P, 2, 512], F32R)
        hl = sb("hl", [P, 2, 512], F32R)

        bank = [ctx.enter_context(nc.psum_tensor(f"ring{i}", [P, 512], F32)) for i in range(RING)]
        num = ctx.enter_context(nc.psum_tensor("num", [P, 512], F32))
        g_ps = ctx.enter_context(nc.psum_tensor("g_ps", [P, 512], F32))
        u_ps = ctx.enter_context(nc.psum_tensor("u_ps", [P, 512], F32))
        d_ps = [ctx.enter_context(nc.psum_tensor(f"d_ps{m}", [P, 512], F32)) for m in range(2)]

        def tile(name):
            return bank[TILES.index(name) % RING]

        load = {n: sem("load_" + n) for n in ("small", "graph", "blocks")}
        x_loaded = sem("x_loaded")
        piece_loaded = [sem(f"piece_loaded{i}") for i in range(2)]
        piece_high = sem("piece_high")
        piece_low = sem("piece_low")
        out_stored = sem("out_stored")
        prep_dve = sem("prep_dve")
        prep_act = sem("prep_act")
        prep_pool = sem("prep_pool")
        prep_pe = sem("prep_pe")
        BI = ["0", "1"]
        filled = Signal(sem("bank_filled"), TILES)
        conv_dve = Signal(sem("conv_by_dve"), (
            [f"bn{q}" for q in range(4)] + [f"ag{q}" for q in range(4)] + ["msq", "m2", "gm", "gsq", "gvar"]
            + [f"xg{q}" for q in range(4)] + ["L00", "L01", "L10", "L11", "Lm", "R", "y000", "M", "y001", "te", "y010",
            "emax", "esub", "esum", "erec", "ET", "y011", "EW", "WE", "y100", "y101", "pb0", "pb1", "y110", "smax0", "y111", "smax1",
            "rinv0", "A00", "A01", "A02", "rinv1", "A10", "A11", "A12"]
            + [f"z{b}{m}" for b in BI for m in BI]
            + ["sum0", "mean0", "sub0", "sum1", "mean1", "sub1", "vs0", "vv0", "vs1", "vv1", "n10", "n20", "n30", "n11", "n21", "n31"]))
        conv_act = Signal(sem("conv_by_act"), (
            ["xT0", "xT1", "y000", "y001", "thE", "y010", "expE", "y011", "y100", "l2", "r2", "y101", "th0", "th1", "y110", "ex00", "ex01", "y111",
             "ex10", "ex11", "sg0", "sg1", "relu0", "relu1", "sq0", "sq1"]))
        conv_pool = Signal(sem("conv_by_pool"), ["rstd", "xb", "vr0", "vr1"])
        norm_names = [f"bs{q}" for q in range(4)] + [f"ba{q}" for q in range(4)] + ["ve"] + [f"nm{q}" for q in range(4)] + ["lo0", "lo1"]
        attn_dve = Signal(sem("attn_by_dve"), norm_names + [
            "kmin0", "k0", "kmin1", "k1", "scan00", "scan01", "scan10", "scan11", "qmin0", "q0", "zq0", "qmin1", "q1", "zq1", "kvm", "da", "dr"]
            + [f"{n}" for n in SCORES[:8]] + ["at0"] + [f"{n}" for n in SCORES[8:]] + ["at1", "x20", "x21"])
        attn_act = Signal(sem("attn_by_act"), ["hi0", "hi1", "ek0", "ek1", "eq0", "eq1", "qe0", "qo0", "qe1", "qo1",
                                               "ve0", "vo0", "ve1", "vo1", "kt", "rdx", "rd0", "rd1"])
        attn_pool = Signal(sem("attn_by_pool"), ["rstd"])
        route_dve = Signal(sem("route_by_dve"), norm_names + [
            "one", "sig", "sb", "p1", "p2", "p3", "gs"] + [f"gx{q}" for q in range(4)] + ["gt"] + [f"gr{q}" for q in range(4)]
            + ["gn", "es"] + [f"ex{q}" for q in range(4)] + ["et"] + [f"er{q}" for q in range(4)]
            + ["ws", "wsum", "weps", "wrec", "wn", "wh", "wl"])
        route_act = Signal(sem("route_by_act"), ["hi0", "hi1", "lg", "eneg", "cb"])
        route_pool = Signal(sem("route_by_pool"), ["rstd"])
        pv_done = Signal(sem("pv_by_pe"), SCORES)
        ffn_pe = Signal(sem("ffn_by_pe"), [f"{k}{j}" for k, j in sum(([("g", j), ("u", j)] if k == "gu" else [(k, j)] for k, j in ffn_steps() if k != "out"), [])])
        fd = []
        fa = []
        for k, j in ffn_steps():
            if k == "gu":
                fd.append(f"h{j}")
                fa.append(f"si{j}")
            if k == "cm":
                fd.append(f"w{j}")
            if k == "cm" or k == "gu" and j >= ROUTED:
                fd.append(f"lo{j}")
                fa.append(f"hi{j}")
            if k == "out":
                fd += ["out0", "out1"]
        ffn_dve = Signal(sem("ffn_by_dve"), fd, start=1)
        ffn_act = Signal(sem("ffn_by_act"), fa)
        x2_kept = Signal(sem("x2_kept_by_pool"), ["x2k"])

        READ_OUT = {"gn": [(conv_dve, "gm")], "R": [(conv_dve, "R")], "M": [(conv_dve, "M")], "prod": [(conv_dve, "te")],
                    "Epre": [(conv_dve, "esub")], "Erep": [(conv_dve, "WE")], "lr": [(conv_act, "r2")],
                    "kt": [(attn_act, "kt")], "kv": [(attn_dve, "kvm")], "dent": [(attn_dve, "da")],
                    "lg": [(route_act, "lg")], "rt": [(route_act, "eneg")], "cb": [(route_act, "cb")]}
        for b in BI:
            READ_OUT["xT" + b] = [(conv_act, "xT" + b)]
            READ_OUT["p2_" + b] = [(conv_dve, "pb" + b)]
            READ_OUT["sp" + b] = [(conv_act, f"ex{b}1")]
            READ_OUT["st" + b] = [(conv_dve, f"A{b}2")]
            READ_OUT["o" + b] = [(conv_act, "sg" + b)]
            READ_OUT["tc" + b] = [(conv_dve, f"z{b}1")]
            READ_OUT["tok" + b] = [(attn_dve, f"nm{2 * int(b) + 1}")]
            READ_OUT["tk" + b] = [(route_dve, f"nm{2 * int(b) + 1}")]
            READ_OUT["xl" + b] = [(attn_dve, "lo" + b)]
            READ_OUT["xn" + b] = [(route_dve, "lo" + b)]
            READ_OUT["q" + b] = [(attn_dve, "q" + b)]
            READ_OUT["k" + b] = [(attn_dve, "k" + b)]
            READ_OUT["v" + b] = [(attn_act, "vo" + b)]
            READ_OUT["rd" + b] = [(attn_act, "rd" + b)]
            READ_OUT["wo" + b] = [(attn_dve, "x2" + b)]
            for m in BI:
                for c in BI:
                    READ_OUT["y" + b + m + c] = [(conv_act, "y" + b + m + c), (conv_dve, "y" + b + m + c)]
        for n in SCORES:
            READ_OUT[n] = [(attn_dve, n)]

        def wait_bank(eng, p, name):
            slot = TILES.index(name)
            slot -= RING
            if slot < 0:
                if isinstance(p, int) and p == 0:
                    return
                slot += SLOTS
                if slot >= len(TILES):
                    slot -= RING
                p = p - 1
            for signal, result in READ_OUT[TILES[slot]]:
                eng.wait_ge(signal.sem, signal.at(p, result))

        def carry(dve):
            dve.memset(carrier[:, 0:1], 0.0)

        def mm3(eng, ps, wh, wl, xh, xl, start, stop):
            eng.matmul(ps, wh, xh, start=start, stop=False)
            eng.matmul(ps, wh, xl, start=False, stop=False)
            return eng.matmul(ps, wl, xh, start=False, stop=stop)

        def run(body):
            eng, front, ffn = body
            for name in FRONT_NAMES:
                front(0, name)
            with eng.Fori(1, PAIRS) as p:
                for kind, what in schedule():
                    if kind == "front":
                        front(p, what)
                    else:
                        ffn(p - 1, kind, what)
            for kind, what in ffn_steps():
                ffn(PAIRS - 1, kind, what)

        PIECES = [(wqkvT.rearrange("(c j) k -> j c k", j=P), wqkv_h[:, :, :], wqkv_l[:, :, :])]
        for w, high, low in ((gateT, gate_h, gate_l), (upT, up_h, up_l)):
            PIECES += [(w[k * P:(k + 1) * P, :], high[:, k, :], low[:, k, :]) for k in range(2)]
        for k in range(2):
            half = slice(k * CHUNKS // 2, (k + 1) * CHUNKS // 2)
            PIECES.append((down[k * FF // 2:(k + 1) * FF // 2, :].rearrange("(c j) n -> j c n", j=P), down_h[:, half, :], down_l[:, half, :]))
        PIECES.append((spread_rows, spread[:, :, :], None))
        SPLIT_AT = ["xT1", "Epre", "lr", "p2_1", "sp1", "st1", "tc1"]

        def piece(i):
            if i == len(PIECES) - 1:
                return scratch[0:32, 1536 * (i % 2):1536 * (i % 2) + 1024].rearrange("p (j m) -> p j m", m=P)
            v = scratch[:, 1536 * (i % 2):1536 * (i % 2) + 1536]
            c = {0: 2, 5: CHUNKS // 2, 6: CHUNKS // 2}.get(i)
            return v.rearrange("p (c n) -> p c n", c=c) if c else v

        block = ctx.enter_context(nc.Block())

        @block.sync
        def _(sp):
            for b in range(2):
                sp.dma_start(x_s[:, b], x_v[0, b]).then_inc(x_loaded, 16)
            sp.dma_start(cs[:, :], consts).then_inc(load["small"], 16)
            sp.dma_start(sm[:, :], small).then_inc(load["small"], 16)
            sp.wait_ge(prep_pool, 2)
            for t in range(8):
                rows = slice(16 * t, 16 * t + 16)
                sp.dma_start(theta_s[rows, :, t, :], theta).then_inc(load["blocks"], 16)
                sp.dma_start(tconv_s[rows, t:t + 3, :], tconv).then_inc(load["blocks"], 16)
            sp.dma_start(vs_s[:, :, :], vsT.rearrange("(c j) k -> j c k", j=P)).then_inc(load["graph"], 16)
            sp.dma_start(bs_s[:, :, :], bsT.rearrange("(c j) k -> j c k", j=P)).then_inc(load["graph"], 16)
            for k in range(3):
                sp.dma_start(cheb_s[:, k], cheb[k].rearrange("(c m) n -> m c n", m=P)).then_inc(load["graph"], 16)
            sp.dma_start(wo_s[:, :, :], woT.rearrange("(c j) k -> j c k", j=P)).then_inc(load["graph"], 16)
            for i, (src, _, _) in enumerate(PIECES):
                if i >= 2:
                    sp.wait_ge(piece_low, i - 1)
                sp.dma_start(piece(i), src).then_inc(piece_loaded[i % 2], 16)

            def prefetch(p, next_pair):
                sp.wait_ge(conv_dve.sem, conv_dve.at(p, "n31"))
                for b in range(2):
                    sp.dma_start(x_s[:, b], x_v[next_pair, b]).then_inc(x_loaded, 16)

            def store(p):
                sp.wait_ge(ffn_dve.sem, ffn_dve.at(p, "out1"))
                for b in range(2):
                    sp.dma_start(out_v[p, b], y_out[:, :, b * L:(b + 1) * L]).then_inc(out_stored, 16)
            prefetch(0, 1)
            with sp.Fori(1, PAIRS - 1) as p:
                prefetch(p, p + 1)
                store(p - 1)
            store(PAIRS - 2)
            store(PAIRS - 1)
            sp.wait_ge(out_stored, 32 * PAIRS + 32)

        @block.gpsimd
        def _(pool):
            pool.memset(theta_s[:, :, :, :], 0.0).then_inc(prep_pool, 1)
            pool.memset(tconv_s[:, :, :], 0.0).then_inc(prep_pool, 1)
            pool.memset(minus_half[:, :], -0.5).then_inc(prep_pool, 1)
            pool.memset(one[:, :], 1.0).then_inc(prep_pool, 1)
            pool.memset(ab[:, :, :], 0.0).then_inc(prep_pool, 1)
            pool.memset(v_s[:, :, :, :, :], 0.0).then_inc(prep_pool, 1)
            pool.memset(gs[:, :, :], FILLER).then_inc(prep_pool, 1)
            pool.memset(gtake[:, :, :], FILLER).then_inc(prep_pool, 1)
            pool.memset(es[:, :, :], FILLER).then_inc(prep_pool, 1)
            pool.memset(etake[:, :, :], FILLER).then_inc(prep_pool, 1)
            pool.wait_ge(prep_pool, 4)
            pool.wait_ge(load["small"], 32)

            def front(p, name):
                if name == "gn":
                    pool.wait_ge(conv_dve.sem, conv_dve.at(p, "gvar"))
                    pool.tensor_tensor(grstd[:, :], gvar[:, :], minus_half[:, 0:4], ALU.pow).then_inc(*conv_pool.mark("rstd"))
                if name == "xT0":
                    pool.wait_ge(conv_dve.sem, conv_dve.at(p, "xg3"))
                    beta = small_at("beta").unsqueeze(1).to_broadcast([P, 64, T])
                    v = x_s[:, :, :, :].rearrange("p b c (f t) -> p (b c f) t", t=T)
                    pool.tensor_tensor(v, v, beta, ALU.add).then_inc(*conv_pool.mark("xb"))
                if name in ("tc0", "tc1"):
                    b = int(name[2])
                    pool.wait_ge(conv_dve.sem, conv_dve.at(p, f"vv{b}"))
                    pool.tensor_tensor(vrstd[:, b], vsum[:, b], minus_half[:, :], ALU.pow).then_inc(*conv_pool.mark(f"vr{b}"))
                if name == "tok1":
                    pool.wait_ge(attn_dve.sem, attn_dve.at(p, "ve"))
                    pool.tensor_tensor(trs[:, :], tve[:, :], minus_half[:, 0:4], ALU.pow).then_inc(*attn_pool.mark("rstd"))
                if name == "tk1":
                    pool.wait_ge(route_dve.sem, route_dve.at(p, "ve"))
                    pool.tensor_tensor(trs[:, :], tve[:, :], minus_half[:, 0:4], ALU.pow).then_inc(*route_pool.mark("rstd"))

            def ffn(p, kind, j):
                if (kind, j) == ("gu", 0):
                    pool.wait_ge(attn_dve.sem, attn_dve.at(p, "x21"))
                    pool.wait_ge(ffn_dve.sem, ffn_dve.at(p, "h0") - 1)
                    pool.tensor_tensor(x2k[:, :, :], x2[:, :, :], one[:, 0:1].unsqueeze(1).to_broadcast([P, 2, 512]), ALU.mult).then_inc(*x2_kept.mark("x2k"))

            run((pool, front, ffn))

        @block.scalar
        def _(act):
            act.wait_ge(load["small"], 32)
            act.wait_ge(prep_dve, 1)
            act.activation(router_h[:, :, 0:16], small_at("router").rearrange("p (c e) -> p c e", c=2), ACT.Copy).then_inc(prep_act, 1)

            def split(i):
                act.wait_ge(piece_loaded[i % 2], 16 * (i // 2 + 1))
                act.activation(PIECES[i][1], piece(i), ACT.Copy).then_inc(piece_high, 1)

            split(0)

            def heads(ps, c):
                return ps.rearrange("p (lc j e) -> p (lc j) e", lc=2, e=32)[:, :, 16 * c:16 * c + 16]

            def front(p, name):
                t = tile(name) if name in TILES else None
                if name in TILES:
                    act_reads = name[:2] in ("xT", "y0", "y1", "lr", "sp", "xl", "xn", "rd", "lg", "rt", "cb", "kt") or name in (
                        "Epre", "o0", "o1", "q0", "q1", "k0", "k1", "v0", "v1")
                    if act_reads and name != "Epre" and name[:2] != "sp":
                        act.wait_ge(filled.sem, filled.at(p, name))
                if name in ("xT0", "xT1"):
                    b = int(name[2])
                    act.activation(xT[:, b].rearrange("p c n -> p (c n)"), t[:, :], ACT.Copy).then_inc(*conv_act.mark(name))
                if name[0] == "y":
                    b, m, c = map(int, name[1:])
                    act.activation(y_s[:, b, m, c, :], t[:, 0:384], ACT.Copy).then_inc(*conv_act.mark(name))
                if name == "prod":
                    act.wait_ge(conv_dve.sem, conv_dve.at(p, "te"))
                    act.activation(te[:, :, :], te[:, :, :], ACT.Tanh, scale=0.5).then_inc(*conv_act.mark("thE"))
                if name == "Epre":
                    act.wait_ge(conv_dve.sem, conv_dve.at(p, "esub"))
                    act.activation(eT[:, :, :], eT[:, :, :], ACT.Exp).then_inc(*conv_act.mark("expE"))
                if name == "lr":
                    act.activation(l2[:, :], t[0:16, :], ACT.Copy).then_inc(*conv_act.mark("l2"))
                    act.activation(r2[:, :], t[32:48, :], ACT.Copy).then_inc(*conv_act.mark("r2"))
                if name in ("p2_0", "p2_1"):
                    b = int(name[3])
                    act.wait_ge(conv_dve.sem, conv_dve.at(p, f"pb{b}"))
                    act.activation(th[:, b], th[:, b], ACT.Tanh, scale=0.5).then_inc(*conv_act.mark(f"th{b}"))
                if name in ("sp0", "sp1"):
                    b = int(name[2])
                    act.wait_ge(conv_dve.sem, conv_dve.at(p, f"smax{b}"))
                    for kc in range(2):
                        act.activation(sT[:, b, kc, :], t[:, kc * N:(kc + 1) * N], ACT.Exp, bias=smax[:, b, kc:kc + 1],
                                       accum_out=ssum[:, b, kc:kc + 1]).then_inc(*conv_act.mark(f"ex{b}{kc}"))
                if name in ("o0", "o1"):
                    b = int(name[1])
                    act.activation(sg[:, b].rearrange("p c n -> p (c n)"), t[:, :], ACT.Relu).then_inc(*conv_act.mark(f"sg{b}"))
                if name == "tc1":
                    for b in range(2):
                        act.wait_ge(conv_dve.sem, conv_dve.at(p, f"z{b}1"))
                        act.activation(z[:, b], z[:, b], ACT.Relu).then_inc(*conv_act.mark(f"relu{b}"))
                    for b in range(2):
                        act.wait_ge(conv_dve.sem, conv_dve.at(p, f"sub{b}"))
                        act.activation(zsq[:, b], z[:, b], ACT.Square).then_inc(*conv_act.mark(f"sq{b}"))
                if name in ("xl0", "xl1"):
                    c = int(name[2])
                    act.activation(xa_h[:, c, :], t[:, :], ACT.Copy).then_inc(*attn_act.mark(f"hi{c}"))
                if name in ("k0", "k1", "q0", "q1"):
                    c = int(name[1])
                    if name[0] == "q":
                        act.wait_ge(attn_dve.sem, attn_dve.at(p, f"k{c}"))
                    act.activation(e_s[:, c, :], t[:, :], ACT.Exp).then_inc(*attn_act.mark("e" + name))
                if name == "q1":
                    for c in range(2):
                        act.wait_ge(attn_dve.sem, attn_dve.at(p, f"q{c}"))
                        act.activation(q_e[:, c, :], q_f[:, c, :], ACT.Copy, scale=const_at("even")).then_inc(*attn_act.mark(f"qe{c}"))
                        act.activation(q_o[:, c, :], q_f[:, c, :], ACT.Copy, scale=const_at("odd")).then_inc(*attn_act.mark(f"qo{c}"))
                if name in ("v0", "v1"):
                    b = int(name[1])
                    act.activation(v_s[:, b].rearrange("p c j e -> p (c j) e")[:, :, 0:16], heads(t[:, :], 0), ACT.Copy).then_inc(*attn_act.mark(f"ve{b}"))
                    act.activation(v_s[:, b].rearrange("p c j e -> p (c j) e")[:, :, 32:48], heads(t[:, :], 1), ACT.Copy).then_inc(*attn_act.mark(f"vo{b}"))
                if name == "kt":
                    act.activation(ktok[:, :], t[:, :], ACT.Copy).then_inc(*attn_act.mark("kt"))
                if name == "dent":
                    act.wait_ge(attn_dve.sem, attn_dve.at(p, "dr"))
                    act.activation(rdx.rearrange("p q h e -> p (q h) e"), rd[:, :, :].rearrange("p q h -> p (q h)").unsqueeze(2).to_broadcast([P, 64, T]),
                                   ACT.Copy).then_inc(*attn_act.mark("rdx"))
                if name in ("rd0", "rd1"):
                    c = int(name[2])
                    act.activation(rd_s[:, c, :], t[:, :], ACT.Copy).then_inc(*attn_act.mark(name))
                if name in ("xn0", "xn1"):
                    c = int(name[2])
                    act.activation(xf_h[:, c, :], t[:, :], ACT.Copy).then_inc(*route_act.mark(f"hi{c}"))
                if name == "lg":
                    act.activation(lgT[:, :], t[0:EXPERTS, :], ACT.Copy).then_inc(*route_act.mark("lg"))
                if name == "rt":
                    act.activation(sc[:, :, :].rearrange("p q e -> p (q e)"), t[:, 0:64], ACT.Exp, scale=-1.0).then_inc(*route_act.mark("eneg"))
                if name == "cb":
                    act.activation(comb[:, :], t[0:32, :], ACT.Copy).then_inc(*route_act.mark("cb"))
                if isinstance(p, int) and name in SPLIT_AT:
                    split(SPLIT_AT.index(name) + 1)

            def ffn(p, kind, j):
                if kind == "gu":
                    act.wait_ge(ffn_pe.sem, ffn_pe.at(p, f"g{j}"))
                    act.activation(sl, g_ps[:, :], ACT.Silu).then_inc(*ffn_act.mark(f"si{j}"))
                if kind == "cm" or kind == "gu" and j >= ROUTED:
                    act.wait_ge(ffn_dve.sem, ffn_dve.at(p, f"w{j}" if j < ROUTED else f"h{j}"))
                    act.activation(hh[:, j % 2, :], hb, ACT.Copy).then_inc(*ffn_act.mark(f"hi{j}"))

            run((act, front, ffn))

        @block.vector
        def _(dve):
            dve.memset(carrier[:, 0:1], 0.0).then_inc(ffn_dve.sem, 1)
            dve.memset(carrier[:, 1:2], 0.0).then_inc(out_stored, 32)
            dve.memset(router_h[:, :, :].bitcast(F32), 0.0).then_inc(prep_dve, 1)
            dve.memset(router_l[:, :, :].bitcast(F32), 0.0).then_inc(prep_dve, 1)
            dve.wait_ge(load["small"], 32)
            dve.tensor_scalar(u3blk[:, :], const_at("diag8"), small_at("u3"), None, ALU.mult).then_inc(prep_dve, 1)
            dve.tensor_scalar(ve_h[:, :, :], small_at("ve", T).unsqueeze(1).to_broadcast([T, 4, T]), 0.5, None, ALU.mult).then_inc(prep_dve, 1)
            dve.tensor_copy(iw1[:, 0:16], const_at("ident", T)[:, 0:16]).then_inc(prep_dve, 1)
            dve.tensor_copy(iw1[:, 16:17], small_at("w1", T)).then_inc(prep_dve, 1)
            dve.tensor_copy(iw1[:, 17:18], small_at("w1", T)).then_inc(prep_dve, 1)
            dve.tensor_tensor(biasy[:, :], small_at("tb"), small_at("rb"), ALU.add).then_inc(prep_dve, 1)
            dve.wait_ge(load["graph"], 96)
            dve.tensor_scalar(vs_s[:, :, :], vs_s[:, :, :], 0.5, None, ALU.mult).then_inc(prep_dve, 1)
            dve.wait_ge(prep_act, 1)
            dve.wait_ge(prep_dve, 2)
            dve.tensor_tensor(router_l[:, :, 0:16], small_at("router").rearrange("p (c e) -> p c e", c=2),
                              router_h[:, :, 0:16].bitcast(F32), ALU.subtract).then_inc(prep_dve, 1)
            dve.wait_ge(prep_dve, 10)
            dve.wait_ge(prep_pool, 10)

            def split(i):
                _, high, low = PIECES[i]
                if low is not None:
                    dve.wait_ge(piece_high, i + 1)
                    dve.tensor_tensor(low, piece(i), high.bitcast(F32), ALU.subtract).then_inc(piece_low, 1)

            split(0)

            def layer_stats(p, sig, t, b):
                for lc in range(2):
                    q = 2 * b + lc
                    dve.bn_stats(tst[:, q, :], t[:, lc * N:(lc + 1) * N]).then_inc(*sig.mark(f"bs{q}"))

            def layer_norm(p, sig, pool_sig, tiles):
                dve.wait_ge(sig.sem, sig.at(p, "bs3"))
                carry(dve)
                for q in range(4):
                    dve.bn_aggr(tmv[:, q, :], tst[:, q, :]).then_inc(*sig.mark(f"ba{q}"))
                dve.wait_ge(sig.sem, sig.at(p, "ba3"))
                dve.tensor_scalar(tve[:, :], tmv[:, :, 1], 1e-5, None, ALU.add).then_inc(*sig.mark("ve"))
                dve.wait_ge(pool_sig.sem, pool_sig.at(p, "rstd"))
                for q in range(4):
                    dve.tensor_scalar(xt[:, q // 2, q % 2, :], tile(tiles[q // 2])[:, (q % 2) * N:(q % 2 + 1) * N],
                                      tmv[:, q, 0:1], trs[:, q:q + 1], ALU.subtract, ALU.mult).then_inc(*sig.mark(f"nm{q}"))

            def own(sig, p, name):
                dve.wait_ge(sig.sem, sig.at(p, name))

            def front(p, name):
                cv, at, rt = conv_dve, attn_dve, route_dve
                t = tile(name) if name in TILES else None
                if name in TILES:
                    dve.wait_ge(filled.sem, filled.at(p, name)) if name not in ("gn",) and name[:2] not in ("xT", "o0", "o1", "lr", "v0", "v1", "kt", "rd", "lg", "cb", "st") and name not in ("rt",) else None
                if name == "gn":
                    dve.wait_ge(x_loaded, 32 * p + 32)
                    for q in range(4):
                        dve.bn_stats(stats[:, q, :], x_s[:, q // 2, q % 2, :]).then_inc(*cv.mark(f"bn{q}"))
                    own(cv, p, "bn3")
                    carry(dve)
                    for q in range(4):
                        dve.bn_aggr(mv[:, q, :], stats[:, q, :]).then_inc(*cv.mark(f"ag{q}"))
                    own(cv, p, "ag3")
                    dve.tensor_tensor(gsq[:, :], mv[:, :, 0], mv[:, :, 0], ALU.mult).then_inc(*cv.mark("msq"))
                    own(cv, p, "msq")
                    dve.tensor_tensor(mv[:, :, 1], mv[:, :, 1], gsq[:, :], ALU.add).then_inc(*cv.mark("m2"))
                    dve.wait_ge(filled.sem, filled.at(p, "gn"))
                    dve.tensor_copy(gmv[:, :, :].rearrange("p q s -> p (q s)"), t[:, 0:8]).then_inc(*cv.mark("gm"))
                    own(cv, p, "gm")
                    dve.tensor_tensor(gsq[:, :], gmv[:, :, 0], gmv[:, :, 0], ALU.mult).then_inc(*cv.mark("gsq"))
                    own(cv, p, "gsq")
                    dve.scalar_tensor_tensor(gvar[:, :], gmv[:, :, 1], 1e-5, gsq[:, :], ALU.add, ALU.subtract).then_inc(*cv.mark("gvar"))
                    dve.wait_ge(conv_pool.sem, conv_pool.at(p, "rstd"))
                    for q in range(4):
                        dve.tensor_scalar(xg[:, q // 2, q % 2, :].rearrange("p (t f) -> p t f", t=T),
                                          x_s[:, q // 2, q % 2, :].rearrange("p (f t) -> p t f", t=T), gmv[:, q, 0:1], grstd[:, q:q + 1],
                                          ALU.subtract, ALU.mult).then_inc(*cv.mark(f"xg{q}"))
                if name == "xT1":
                    for b in range(2):
                        dve.wait_ge(conv_act.sem, conv_act.at(p, f"xT{b}"))
                        for c in range(2):
                            if b or c:
                                own(cv, p, ["L00", "L01", "L10"][2 * b + c - 1])
                            dve.tensor_tensor_reduce(junk[:, :], xT[:, b, c, :], small_at("u1"), 1.0, 0.0, ALU.mult, ALU.add,
                                                     lsum[:, b, c:c + 1]).then_inc(*cv.mark(f"L{b}{c}"))
                    own(cv, p, "L11")
                    dve.tensor_tensor(lm[:, :, :, :], const_at("halves").rearrange("p (c t) -> p c t", c=2).unsqueeze(1).to_broadcast([P, 2, 2, T]),
                                      lsum[:, :, :].unsqueeze(3).to_broadcast([P, 2, 2, T]), ALU.mult).then_inc(*cv.mark("Lm"))
                if name == "R":
                    dve.tensor_copy(r_s[:, :, :, :].rearrange("p m b s -> p b m s"), t[:, 0:64].rearrange("p (b m s) -> p b m s", b=2, m=2)).then_inc(*cv.mark("R"))
                if name == "M":
                    dve.tensor_copy(m_s[:, :], t[:, 0:32]).then_inc(*cv.mark("M"))
                if name[0] == "y":
                    b, m, c = map(int, name[1:])
                    dve.wait_ge(conv_act.sem, conv_act.at(p, name))
                    dve.tensor_tensor(resb[:, b, m, c * P:(c + 1) * P].rearrange("p (t o) -> p t o", o=T),
                                      t[:, 384:512].rearrange("p (t o) -> p t o", o=T),
                                      biasy[:, :].unsqueeze(1).to_broadcast([P, 8, T]), ALU.add).then_inc(*cv.mark(name))
                if name == "prod":
                    dve.tensor_tensor(te[:, :, :], t[0:T, 0:32].rearrange("p (b s) -> p b s", b=2),
                                      small_at("be", T).unsqueeze(1).to_broadcast([T, 2, T]), ALU.add).then_inc(*cv.mark("te"))
                if name == "Epre":
                    e = t[0:T, 0:32].rearrange("p (b s) -> p b s", b=2)
                    dve.tensor_reduce(emax[:, :], e, AX.X, ALU.max).then_inc(*cv.mark("emax"))
                    own(cv, p, "emax")
                    dve.tensor_tensor(eT[:, :, :], e, emax[:, :].unsqueeze(2).to_broadcast([T, 2, T]), ALU.subtract).then_inc(*cv.mark("esub"))
                    dve.wait_ge(conv_act.sem, conv_act.at(p, "expE"))
                    dve.tensor_reduce(esum[:, :], eT[:, :, :], AX.X, ALU.add).then_inc(*cv.mark("esum"))
                    own(cv, p, "esum")
                    dve.reciprocal(emax[:, :], esum[:, :]).then_inc(*cv.mark("erec"))
                    own(cv, p, "erec")
                    dve.tensor_tensor(eTx, eT[:, :, :].unsqueeze(3).to_broadcast([T, 2, T, T]),
                                      emax[:, :].unsqueeze(2).to_broadcast([T, 2, T]).unsqueeze(3).to_broadcast([T, 2, T, T]), ALU.mult).then_inc(*cv.mark("ET"))
                if name == "Erep":
                    e = t[:, 0:128].rearrange("p (q s) -> p q s", q=4)
                    dve.tensor_scalar(ab[:, :, 32:48], e[:, :, 0:16], small_at("w3"), None, ALU.mult).then_inc(*cv.mark("EW"))
                    dve.tensor_tensor(ab[:, :, 0:16], small_at("w2").unsqueeze(1).to_broadcast([P, 4, T]), e[:, :, 16:17].to_broadcast([P, 4, T]), ALU.mult).then_inc(*cv.mark("WE"))
                if name in ("p2_0", "p2_1"):
                    b = int(name[3])
                    dve.tensor_tensor(th[:, b].rearrange("p c n -> p (c n)"), t[:, :], bs_s[:, :, :].rearrange("p c n -> p (c n)"), ALU.add).then_inc(*cv.mark(f"pb{b}"))
                if name in ("sp0", "sp1"):
                    b = int(name[2])
                    dve.tensor_reduce(smax[:, b, :], t[:, :].rearrange("p (c n) -> p c n", c=2), AX.X, ALU.max, negate=True).then_inc(*cv.mark(f"smax{b}"))
                if name in ("st0", "st1"):
                    b = int(name[2])
                    dve.wait_ge(conv_act.sem, conv_act.at(p, f"ex{b}1"))
                    dve.reciprocal(rinv[:, b, :], ssum[:, b, :]).then_inc(*cv.mark(f"rinv{b}"))
                    dve.wait_ge(filled.sem, filled.at(p, name))
                    for k in range(3):
                        dve.tensor_tensor(a_s[b][:, k].rearrange("p c n -> p (c n)"), t[:, :], cheb_s[:, k].rearrange("p c n -> p (c n)"), ALU.mult).then_inc(*cv.mark(f"A{b}{k}"))
                if name in ("tc0", "tc1"):
                    b = int(name[2])
                    for m in range(2):
                        dve.scalar_tensor_tensor(z[:, b, m, :], t[:, m * 256:(m + 1) * 256], rinv[:, b, m:m + 1], resb[:, b, m, :], ALU.mult, ALU.add).then_inc(*cv.mark(f"z{b}{m}"))
                if name == "tc1":
                    def by_time(v):
                        return v.rearrange("p m (t o) -> p m o t", o=T)
                    def per_row(v):
                        return v.rearrange("p (m o) -> p m o", m=2).unsqueeze(2).to_broadcast([P, 2, T, T])
                    for b in range(2):
                        dve.wait_ge(conv_act.sem, conv_act.at(p, f"relu{b}"))
                        dve.tensor_reduce(msum[:, b].rearrange("p (m o) -> p m o", m=2), by_time(z[:, b]), AX.X, ALU.add).then_inc(*cv.mark(f"sum{b}"))
                        own(cv, p, f"sum{b}")
                        dve.tensor_scalar(msum[:, b], msum[:, b], 1.0 / T, None, ALU.mult).then_inc(*cv.mark(f"mean{b}"))
                        own(cv, p, f"mean{b}")
                        zb = z[:, b].rearrange("p m (t o) -> p m t o", o=T)
                        dve.tensor_tensor(zb, zb, per_row(msum[:, b]), ALU.subtract).then_inc(*cv.mark(f"sub{b}"))
                    for b in range(2):
                        dve.wait_ge(conv_act.sem, conv_act.at(p, f"sq{b}"))
                        dve.tensor_reduce(vsum[:, b].rearrange("p (m o) -> p m o", m=2), by_time(zsq[:, b]), AX.X, ALU.add).then_inc(*cv.mark(f"vs{b}"))
                        own(cv, p, f"vs{b}")
                        dve.tensor_scalar(vsum[:, b], vsum[:, b], 1.0 / T, 1e-5, ALU.mult, ALU.add).then_inc(*cv.mark(f"vv{b}"))
                    for b in range(2):
                        dve.wait_ge(conv_pool.sem, conv_pool.at(p, f"vr{b}"))
                        zb = z[:, b].rearrange("p m (t o) -> p m t o", o=T)
                        dve.tensor_tensor(zb, zb, per_row(vrstd[:, b]), ALU.mult).then_inc(*cv.mark(f"n1{b}"))
                        own(cv, p, f"n1{b}")
                        zt = z[:, b].rearrange("p m (t o) -> p (m t) o", o=T)
                        gm = small_at("gamma").unsqueeze(1).to_broadcast([P, 2, T]).unsqueeze(3).to_broadcast([P, 2, T, T])
                        dve.tensor_tensor(zb, zb, gm, ALU.mult).then_inc(*cv.mark(f"n2{b}"))
                        own(cv, p, f"n2{b}")
                        dve.tensor_tensor(x1[:, :, b, :].rearrange("p m (o t) -> p m o t", t=T), by_time(z[:, b]),
                                          x_s[:, b].rearrange("p m (o t) -> p m o t", t=T), ALU.add).then_inc(*cv.mark(f"n3{b}"))
                if name in ("tok0", "tok1"):
                    layer_stats(p, at, t, int(name[3]))
                    if name == "tok1":
                        layer_norm(p, at, attn_pool, ["tok0", "tok1"])
                if name in ("xl0", "xl1"):
                    c = int(name[2])
                    dve.wait_ge(attn_act.sem, attn_act.at(p, f"hi{c}"))
                    dve.tensor_tensor(xa_l[:, c, :], t[:, :], xa_h[:, c, :].bitcast(F32), ALU.subtract).then_inc(*at.mark(f"lo{c}"))
                if name in ("k0", "k1", "q0", "q1"):
                    c = int(name[1])
                    f = q_f if name[0] == "q" else k_f
                    dve.wait_ge(attn_act.sem, attn_act.at(p, "e" + name))
                    dve.tensor_scalar(e_s[:, c, :], e_s[:, c, :], 1.0, None, ALU.min).then_inc(*at.mark(f"{name[0]}min{c}"))
                    own(at, p, f"{name[0]}min{c}")
                    dve.scalar_tensor_tensor(f[:, c, :], t[:, :], 0.0, e_s[:, c, :], ALU.max, ALU.add).then_inc(*at.mark(name))
                if name == "k1":
                    for c in range(2):
                        own(at, p, f"k{c}")
                        for b in range(2):
                            k_b = k_f[:, c, b * L:(b + 1) * L]
                            dve.tensor_tensor_scan(zs[:, c, b * L:(b + 1) * L], k_b, k_b, 0.0, ALU.add, ALU.max).then_inc(*at.mark(f"scan{c}{b}"))
                if name in ("q0", "q1"):
                    c = int(name[1])
                    own(at, p, name)
                    dve.tensor_tensor(zs[:, c, :], zs[:, c, :], q_f[:, c, :], ALU.mult).then_inc(*at.mark(f"zq{c}"))
                if name == "kv":
                    dve.tensor_tensor(kvm[:, :].rearrange("p (q e) -> p q e", q=4), t[:, :].rearrange("p (q e) -> p q e", q=4),
                                      const_at("heads16").unsqueeze(1).to_broadcast([P, 4, P]), ALU.mult).then_inc(*at.mark("kvm"))
                if name == "dent":
                    dve.tensor_scalar(rd[:, :, :].rearrange("p q h -> p (q h)"), t[:, 0:64], 1e-5, None, ALU.add).then_inc(*at.mark("da"))
                    own(at, p, "da")
                    dve.reciprocal(rd[:, :, :], rd[:, :, :]).then_inc(*at.mark("dr"))
                if name in ("P0", "P1"):
                    b = int(name[1])
                    for n in SCORES[8 * b:8 * b + 8]:
                        i = SCORES.index(n)
                        if i >= 3:
                            dve.wait_ge(pv_done.sem, pv_done.at(p, SCORES[i - 3]))
                        dve.wait_ge(filled.sem, filled.at(p, n))
                        dve.tensor_tensor(p_s[:, i % 3, :].rearrange("p (h l) -> p h l", h=4), tile(n)[:, :].rearrange("p (h l) -> p h l", h=4),
                                          const_at("causal").unsqueeze(1).to_broadcast([P, 4, P]), ALU.mult).then_inc(*at.mark(n))
                    dve.wait_ge(pv_done.sem, pv_done.at(p, SCORES[8 * b + 7]))
                    dve.wait_ge(attn_act.sem, attn_act.at(p, "rd1"))
                    dve.tensor_tensor(attn[:, :, b * L:(b + 1) * L], num[:, :].rearrange("p (c l) -> p c l", c=2),
                                      rd_s[:, :, b * L:(b + 1) * L], ALU.mult).then_inc(*at.mark(f"at{b}"))
                if name in ("wo0", "wo1"):
                    c = int(name[2])
                    if c == 0 and not isinstance(p, int):
                        dve.wait_ge(x2_kept.sem, x2_kept.at(p - 1, "x2k"))
                    dve.scalar_tensor_tensor(x2[:, c, :], t[:, :], small_at("bo")[:, c:c + 1], x1[:, c].rearrange("p b l -> p (b l)"),
                                             ALU.add, ALU.add).then_inc(*at.mark(f"x2{c}"))
                if name in ("tk0", "tk1"):
                    layer_stats(p, rt, t, int(name[2]))
                    if name == "tk1":
                        layer_norm(p, rt, route_pool, ["tk0", "tk1"])
                if name in ("xn0", "xn1"):
                    c = int(name[2])
                    dve.wait_ge(route_act.sem, route_act.at(p, f"hi{c}"))
                    dve.tensor_tensor(xf_l[:, c, :], t[:, :], xf_h[:, c, :].bitcast(F32), ALU.subtract).then_inc(*rt.mark(f"lo{c}"))
                if name == "rt":
                    route(p)
                if isinstance(p, int) and name in SPLIT_AT:
                    split(SPLIT_AT.index(name) + 1)

            def route(p):
                rt = route_dve
                dve.wait_ge(route_act.sem, route_act.at(p, "eneg"))
                dve.tensor_scalar(sc[:, :, :], sc[:, :, :], 1.0, None, ALU.add).then_inc(*rt.mark("one"))
                own(rt, p, "one")
                dve.reciprocal(sc[:, :, :], sc[:, :, :]).then_inc(*rt.mark("sig"))
                own(rt, p, "sig")
                dve.tensor_tensor(scb[:, :, :], sc[:, :, :], small_at("corr").unsqueeze(1).to_broadcast([P, 4, EXPERTS]), ALU.add).then_inc(*rt.mark("sb"))
                own(rt, p, "sb")
                g = scb[:, :, :].rearrange("p q (g e) -> p (q g) e", e=4)
                dve.tensor_tensor(pairs[:, :, 0:3], g[:, :, 0:3], g[:, :, 1:4], ALU.add).then_inc(*rt.mark("p1"))
                dve.tensor_tensor(pairs[:, :, 3:5], g[:, :, 0:2], g[:, :, 2:4], ALU.add).then_inc(*rt.mark("p2"))
                dve.tensor_tensor(pairs[:, :, 5:6], g[:, :, 0:1], g[:, :, 3:4], ALU.add).then_inc(*rt.mark("p3"))
                own(rt, p, "p3")
                dve.tensor_reduce(gs[:, :, 0:4], pairs[:, :, :].rearrange("p (q g) s -> p q g s", q=4), AX.X, ALU.max).then_inc(*rt.mark("gs"))
                own(rt, p, "gs")
                carry(dve)
                for q in range(4):
                    dve.max(gtop[:, q, :], gs[:, q, :]).then_inc(*rt.mark(f"gx{q}"))
                own(rt, p, "gx3")
                dve.tensor_copy(gtake[:, :, 0:2], gtop[:, :, 0:2]).then_inc(*rt.mark("gt"))
                own(rt, p, "gt")
                carry(dve)
                for q in range(4):
                    dve.match_replace(gmark[:, q, :], gtake[:, q, :], gs[:, q, :], BIG).then_inc(*rt.mark(f"gr{q}"))
                own(rt, p, "gr3")
                dve.tensor_scalar(gneg[:, :, :], gmark[:, :, 0:4], BIG / 2, UNCHOSEN, ALU.is_lt, ALU.mult).then_inc(*rt.mark("gn"))
                own(rt, p, "gn")
                dve.tensor_tensor(es[:, :, 0:16].rearrange("p q (g e) -> p q g e", e=4), scb[:, :, :].rearrange("p q (g e) -> p q g e", e=4),
                                  gneg[:, :, :].unsqueeze(3).to_broadcast([P, 4, 4, 4]), ALU.add).then_inc(*rt.mark("es"))
                own(rt, p, "es")
                carry(dve)
                for q in range(4):
                    dve.max(etop[:, q, :], es[:, q, 0:16]).then_inc(*rt.mark(f"ex{q}"))
                own(rt, p, "ex3")
                dve.tensor_copy(etake[:, :, 0:4], etop[:, :, 0:4]).then_inc(*rt.mark("et"))
                own(rt, p, "et")
                carry(dve)
                for q in range(4):
                    dve.match_replace(emark[:, q, :], etake[:, q, :], es[:, q, :], BIG).then_inc(*rt.mark(f"er{q}"))
                own(rt, p, "er3")
                dve.scalar_tensor_tensor(wsel[:, :, :], emark[:, :, 0:16], BIG / 2, sc[:, :, :], ALU.is_ge, ALU.mult).then_inc(*rt.mark("ws"))
                own(rt, p, "ws")
                dve.tensor_reduce(wsum[:, :], wsel[:, :, :], AX.X, ALU.add).then_inc(*rt.mark("wsum"))
                own(rt, p, "wsum")
                dve.tensor_scalar(wsum[:, :], wsum[:, :], 1e-20, None, ALU.add).then_inc(*rt.mark("weps"))
                own(rt, p, "weps")
                dve.reciprocal(wsum[:, :], wsum[:, :]).then_inc(*rt.mark("wrec"))
                own(rt, p, "wrec")
                dve.tensor_tensor(wsel[:, :, :], wsel[:, :, :], wsum[:, :].unsqueeze(2).to_broadcast([P, 4, EXPERTS]), ALU.mult).then_inc(*rt.mark("wn"))
                own(rt, p, "wn")
                dve.tensor_copy(whl[:, :, 0, :], wsel[:, :, :]).then_inc(*rt.mark("wh"))
                own(rt, p, "wh")
                dve.tensor_tensor(whl[:, :, 1, :], wsel[:, :, :], whl[:, :, 0, :].bitcast(F32), ALU.subtract).then_inc(*rt.mark("wl"))

            def ffn(p, kind, j):
                if kind == "gu":
                    dve.wait_ge(ffn_pe.sem, ffn_pe.at(p, f"u{j}"))
                    dve.wait_ge(ffn_act.sem, ffn_act.at(p, f"si{j}"))
                    dve.wait_ge(ffn_dve.sem, ffn_dve.at(p, f"h{j}") - 1)
                    dve.tensor_tensor(hb, sl, u_ps[:, :], ALU.mult).then_inc(*ffn_dve.mark(f"h{j}"))
                if kind == "cm":
                    dve.wait_ge(ffn_pe.sem, ffn_pe.at(p, f"cm{j}"))
                    dve.wait_ge(ffn_dve.sem, ffn_dve.at(p, f"h{j}"))
                    dve.tensor_tensor(hb, hb, g_ps[:, :], ALU.mult).then_inc(*ffn_dve.mark(f"w{j}"))
                if kind == "cm" or kind == "gu" and j >= ROUTED:
                    dve.wait_ge(ffn_act.sem, ffn_act.at(p, f"hi{j}"))
                    dve.tensor_tensor(hl[:, j % 2, :], hb, hh[:, j % 2, :].bitcast(F32), ALU.subtract).then_inc(*ffn_dve.mark(f"lo{j}"))
                if kind == "out":
                    dve.wait_ge(ffn_pe.sem, ffn_pe.at(p, f"dn{CHUNKS - 1}"))
                    dve.wait_ge(x2_kept.sem, x2_kept.at(p, "x2k"))
                    dve.wait_ge(out_stored, 32 * p + 32)
                    for m in range(2):
                        dve.tensor_tensor(y_out[:, m, :], d_ps[m][:, :], x2k[:, m, :], ALU.add).then_inc(*ffn_dve.mark(f"out{m}"))

            run((dve, front, ffn))

        @block.tensor
        def _(pe):
            pe.wait_ge(load["small"], 32)
            pe.wait_ge(load["blocks"], 256)
            pe.wait_ge(prep_dve, 10)
            pe.wait_ge(prep_pool, 10)
            f32 = filled

            def split_products(t, cols, rhs_h, rhs_l, wh, wl):
                for k in range(2):
                    last = mm3(pe, t, wh[:, k, cols], wl[:, k, cols], rhs_h[:, k, :], rhs_l[:, k, :], k == 0, k == 1)
                return last

            def scores(p, n):
                b, lc, j = map(int, n[1:])
                wait_bank(pe, p, n)
                rows, cols = slice(32 * j, 32 * j + 32), slice(b * L + lc * P, b * L + lc * P + P)
                for c in range(2):
                    for odd in range(2):
                        last = pe.matmul(tile(n)[:, (2 * c + odd) * P:(2 * c + odd + 1) * P], k_f[rows, c, cols],
                                         (q_o if odd else q_e)[rows, c, cols], start=True, stop=True, tile_position=(32 * j, 0))
                last.then_inc(*filled.mark(n))

            def weigh(p, n):
                b, lc, j = map(int, n[1:])
                pe.wait_ge(attn_dve.sem, attn_dve.at(p, n))
                rows = slice(32 * j, 32 * j + 32)
                i = SCORES.index(n)
                for c in range(2):
                    for odd in range(2):
                        last = pe.matmul(num[rows, c * L + lc * P:c * L + lc * P + P], v_s[:, b, lc, 4 * c + j, 16 * odd:16 * odd + 32],
                                         p_s[:, i % 3, (2 * c + odd) * P:(2 * c + odd + 1) * P], start=(lc == 0 and c == 0 and odd == 0),
                                         stop=(odd == 1), skip_group_check=True, tile_position=(0, 32 * j))
                last.then_inc(*pv_done.mark(n))

            def front(p, name):
                t = tile(name) if name in TILES else None
                if name in TILES:
                    wait_bank(pe, p, name)
                if name == "gn":
                    pe.wait_ge(conv_dve.sem, conv_dve.at(p, "m2"))
                    pe.matmul(t[:, 0:8], const_at("mean8"), mv[:, :, :].rearrange("p q s -> p (q s)"), start=True, stop=True).then_inc(*filled.mark(name))
                if name in ("xT0", "xT1"):
                    b = int(name[2])
                    for c in range(2):
                        for m in range(2):
                            if c == 0:
                                pe.wait_ge(conv_dve.sem, conv_dve.at(p, f"xg{2 * b + m}"))
                            last = pe.transpose(t[:, c * N + m * P:c * N + (m + 1) * P], xg[:, b, m, c * P:(c + 1) * P], ident)
                    last.then_inc(*filled.mark(name))
                if name == "R":
                    pe.wait_ge(conv_act.sem, conv_act.at(p, "xT1"))
                    for b in range(2):
                        for m in range(2):
                            for c in range(2):
                                o = (2 * b + m) * 16 + 8 * c
                                last = pe.matmul(t[:, o:o + 8], xT[:, b, c, m * P:(m + 1) * P], u3blk[:, :], start=True, stop=True)
                    last.then_inc(*filled.mark(name))
                if name == "M":
                    pe.wait_ge(conv_dve.sem, conv_dve.at(p, "R"))
                    for m in range(2):
                        last = pe.matmul(t[:, 0:32], small_at("u2")[:, m * P:(m + 1) * P], r_s[:, m].rearrange("p b s -> p (b s)"), start=(m == 0), stop=(m == 1))
                    last.then_inc(*filled.mark(name))
                if name[0] == "y":
                    b, m, c = map(int, name[1:])
                    pe.matmul(t[:, :], xT[:, b, c, m * P:(m + 1) * P], theta_s[:, :, :, :].rearrange("p k t o -> p (k t o)"), start=True, stop=True).then_inc(*filled.mark(name))
                if name == "prod":
                    pe.wait_ge(conv_dve.sem, conv_dve.at(p, "M"))
                    for b in range(2):
                        for c in range(2):
                            last = pe.matmul(t[0:T, b * T:(b + 1) * T], m_s[:, b * T:(b + 1) * T], lm[:, b, c, :], start=(c == 0), stop=(c == 1))
                    last.then_inc(*filled.mark(name))
                if name == "Epre":
                    pe.wait_ge(conv_act.sem, conv_act.at(p, "thE"))
                    pe.matmul(t[0:4 * T, 0:32], ve_h[:, :, :].rearrange("p r s -> p (r s)"), te[:, :, :].rearrange("p b s -> p (b s)"), start=True, stop=True).then_inc(*filled.mark(name))
                if name == "Erep":
                    pe.wait_ge(conv_dve.sem, conv_dve.at(p, "ET"))
                    for b in range(2):
                        for c in range(2):
                            o = (2 * b + c) * 32
                            last = pe.matmul(t[:, o:o + 17], eTx[:, b, 8 * c:8 * c + 8].rearrange("p j f -> p (j f)"), iw1[:, 0:17], start=True, stop=True)
                    last.then_inc(*filled.mark(name))
                if name == "lr":
                    pe.wait_ge(conv_dve.sem, conv_dve.at(p, "WE"))
                    for b in range(2):
                        for c in range(2):
                            last = pe.matmul(t[0:64, b * N:(b + 1) * N], ab[:, 2 * b + c, :], xT[:, b, c, :], start=(c == 0), stop=(c == 1))
                    last.then_inc(*filled.mark(name))
                if name in ("p2_0", "p2_1"):
                    b = int(name[3])
                    pe.wait_ge(conv_act.sem, conv_act.at(p, "r2"))
                    for m in range(2):
                        last = pe.matmul(t[:, m * N:(m + 1) * N], r2[:, b * N + m * P:b * N + (m + 1) * P], l2[:, b * N:(b + 1) * N], start=True, stop=True)
                    last.then_inc(*filled.mark(name))
                if name in ("sp0", "sp1"):
                    b = int(name[2])
                    pe.wait_ge(conv_act.sem, conv_act.at(p, f"th{b}"))
                    for kc in range(2):
                        for jc in range(2):
                            last = pe.matmul(t[:, kc * N:(kc + 1) * N], vs_s[:, jc, kc * P:(kc + 1) * P], th[:, b, jc, :], start=(jc == 0), stop=(jc == 1))
                    last.then_inc(*filled.mark(name))
                if name in ("st0", "st1"):
                    b = int(name[2])
                    pe.wait_ge(conv_act.sem, conv_act.at(p, f"ex{b}1"))
                    for kc in range(2):
                        for ic in range(2):
                            last = pe.transpose(t[:, ic * N + kc * P:ic * N + (kc + 1) * P], sT[:, b, kc, ic * P:(ic + 1) * P], ident)
                    last.then_inc(*filled.mark(name))
                if name in ("o0", "o1"):
                    b = int(name[1])
                    pe.wait_ge(conv_dve.sem, conv_dve.at(p, f"A{b}2"))
                    pe.wait_ge(conv_act.sem, conv_act.at(p, f"y{b}11"))
                    for c in range(2):
                        for k in range(3):
                            for m in range(2):
                                last = pe.matmul(t[:, c * N:(c + 1) * N], y_s[:, b, m, c, k * P:(k + 1) * P], a_s[b][:, k, m, :],
                                                 start=(k == 0 and m == 0), stop=(k == 2 and m == 1))
                    last.then_inc(*filled.mark(name))
                if name in ("tc0", "tc1"):
                    b = int(name[2])
                    pe.wait_ge(conv_act.sem, conv_act.at(p, f"sg{b}"))
                    band = tconv_s[:, :, :].rearrange("p r o -> p (r o)")
                    for m in range(2):
                        pe.matmul(t[:, m * 256:m * 256 + 144], sg[:, b, 0, m * P:(m + 1) * P], band[:, 16:160], start=True, stop=False, skip_group_check=True)
                        last = pe.matmul(t[:, m * 256 + 112:m * 256 + 256], sg[:, b, 1, m * P:(m + 1) * P], band[:, 0:144], start=False, stop=True, skip_group_check=True)
                    last.then_inc(*filled.mark(name))
                if name in ("tok0", "tok1", "tk0", "tk1"):
                    b = int(name[-1])
                    if name[1] == "o":
                        pe.wait_ge(conv_dve.sem, conv_dve.at(p, f"n3{b}"))
                    else:
                        pe.wait_ge(attn_dve.sem, attn_dve.at(p, "x21"))
                    for lc in range(2):
                        for c in range(2):
                            src = x1[:, c, b, lc * P:(lc + 1) * P] if name[1] == "o" else x2[:, c, b * L + lc * P:b * L + (lc + 1) * P]
                            last = pe.transpose(t[:, lc * N + c * P:lc * N + (c + 1) * P], src, ident)
                    last.then_inc(*filled.mark(name))
                if name in ("xl0", "xl1", "xn0", "xn1"):
                    c = int(name[2])
                    sig = attn_dve if name[1] == "l" else route_dve
                    pe.wait_ge(sig.sem, sig.at(p, "nm3"))
                    for q in range(4):
                        last = pe.transpose(t[:, q * P:(q + 1) * P], xt[:, q // 2, q % 2, c * P:(c + 1) * P], ident)
                    last.then_inc(*filled.mark(name))
                if name in ("q0", "q1", "k0", "k1"):
                    c = int(name[1])
                    pe.wait_ge(attn_dve.sem, attn_dve.at(p, "lo1"))
                    o = c * P + (N if name[0] == "k" else 0)
                    split_products(t[:, :], slice(o, o + P), xa_h, xa_l, wqkv_h, wqkv_l).then_inc(*filled.mark(name))
                if name in ("v0", "v1"):
                    b = int(name[1])
                    for lc in range(2):
                        cols = slice(b * L + lc * P, b * L + (lc + 1) * P)
                        for k in range(2):
                            last = mm3(pe, t[:, lc * N:(lc + 1) * N], xa_h[:, k, cols], xa_l[:, k, cols], wqkv_h[:, k, 2 * N:], wqkv_l[:, k, 2 * N:], k == 0, k == 1)
                    last.then_inc(*filled.mark(name))
                if name == "kt":
                    pe.wait_ge(attn_dve.sem, attn_dve.at(p, "k1"))
                    for b in range(2):
                        for c in range(2):
                            last = pe.transpose(t[:, (2 * b + c) * P:(2 * b + c + 1) * P], k_f[:, c, b * L:b * L + P], ident)
                    last.then_inc(*filled.mark(name))
                if name == "kv":
                    pe.wait_ge(attn_act.sem, attn_act.at(p, "kt"))
                    for b in range(2):
                        for c in range(2):
                            q = 2 * b + c
                            for odd in range(2):
                                last = pe.matmul(t[:, q * P:(q + 1) * P], ktok[:, q * P:(q + 1) * P], v_s[:, b, 0, 4 * c:4 * c + 4, 16 * odd:16 * odd + 32],
                                                 start=(odd == 0), stop=(odd == 1))
                    last.then_inc(*filled.mark(name))
                if name == "dent":
                    pe.wait_ge(attn_dve.sem, attn_dve.at(p, "zq1"))
                    for q in range(4):
                        for c in range(2):
                            last = pe.matmul(t[:, q * 16 + 8 * c:q * 16 + 8 * c + 8], zs[:, c, q * P:(q + 1) * P], const_at("head"), start=True, stop=True)
                    last.then_inc(*filled.mark(name))
                if name in ("rd0", "rd1"):
                    c = int(name[2])
                    pe.wait_ge(attn_act.sem, attn_act.at(p, "rdx"))
                    for q in range(4):
                        last = pe.matmul(t[:, q * P:(q + 1) * P], rdx[:, q, 8 * c:8 * c + 8].rearrange("p h e -> p (h e)"), ident, start=True, stop=True)
                    last.then_inc(*filled.mark(name))
                if name in ("P0", "P1"):
                    b = int(name[1])
                    pe.wait_ge(attn_act.sem, attn_act.at(p, "rd1"))
                    pe.wait_ge(attn_dve.sem, attn_dve.at(p, "kvm" if b == 0 else "at0"))
                    mine = SCORES[8 * b:8 * b + 8]
                    scores(p, mine[0])
                    scores(p, mine[1])
                    for i in range(8):
                        if i + 2 < 8:
                            scores(p, mine[i + 2])
                        if i == 4:
                            for c in range(2):
                                pe.matmul(num[:, c * L + P:(c + 1) * L], kvm[:, (2 * b + c) * P:(2 * b + c + 1) * P], q_f[:, c, b * L + P:(b + 1) * L],
                                          start=False, stop=False, skip_group_check=True)
                        weigh(p, mine[i])
                if name in ("wo0", "wo1"):
                    c = int(name[2])
                    pe.wait_ge(attn_dve.sem, attn_dve.at(p, "at1"))
                    for k in range(2):
                        last = pe.matmul(t[:, :], wo_s[:, k, c * P:(c + 1) * P], attn[:, k, :], start=(k == 0), stop=(k == 1))
                    last.then_inc(*filled.mark(name))
                if name == "lg":
                    pe.wait_ge(route_dve.sem, route_dve.at(p, "lo1"))
                    split_products(t[:, :], slice(0, P), xf_h, xf_l, router_h, router_l).then_inc(*filled.mark(name))
                if name == "rt":
                    pe.wait_ge(route_act.sem, route_act.at(p, "lg"))
                    for q in range(4):
                        last = pe.matmul(t[:, q * 16:(q + 1) * 16], lgT[:, q * P:(q + 1) * P], ident[0:16, 0:16], start=True, stop=True)
                    last.then_inc(*filled.mark(name))
                if name == "cb":
                    pe.wait_ge(route_dve.sem, route_dve.at(p, "wl"))
                    for q in range(4):
                        last = pe.transpose(t[0:32, q * P:(q + 1) * P], whl[:, q].rearrange("p s e -> p (s e)").bitcast(F32), ident)
                    last.then_inc(*filled.mark(name))

            def ffn(p, kind, j):
                if kind == "gu":
                    cols = slice(j * P, (j + 1) * P)
                    if j == 0:
                        pe.wait_ge(route_act.sem, route_act.at(p, "cb"))
                        if not isinstance(p, int):
                            pe.wait_ge(piece_low, len(PIECES) - 1)
                            pe.wait_ge(piece_high, len(PIECES))
                    if j:
                        pe.wait_ge(ffn_dve.sem, ffn_dve.at(p, f"w{j - 1}" if j - 1 < ROUTED else f"h{j - 1}"))
                    split_products(g_ps[:, :], cols, xf_h, xf_l, gate_h, gate_l).then_inc(*ffn_pe.mark(f"g{j}"))
                    split_products(u_ps[:, :], cols, xf_h, xf_l, up_h, up_l).then_inc(*ffn_pe.mark(f"u{j}"))
                if kind == "cm":
                    pe.wait_ge(ffn_act.sem, ffn_act.at(p, f"si{j}"))
                    pe.matmul(g_ps[:, :], spread[:, j, :], comb[:, :], start=True, stop=True).then_inc(*ffn_pe.mark(f"cm{j}"))
                if kind == "dn":
                    pe.wait_ge(ffn_dve.sem, ffn_dve.at(p, f"lo{j}"))
                    for m in range(2):
                        last = mm3(pe, d_ps[m][:, :], down_h[:, j, m * P:(m + 1) * P], down_l[:, j, m * P:(m + 1) * P],
                                   hh[:, j % 2, :], hl[:, j % 2, :], j == 0, j == CHUNKS - 1)
                    last.then_inc(*ffn_pe.mark(f"dn{j}"))

            run((pe, front, ffn))


def kernel(**inputs):
    import numpy as _np
    import concourse.bacc as _bacc
    from concourse import mybir as _mybir
    from concourse.bass_utils import run_bass_kernel_spmd as _run

    a = {k: _np.ascontiguousarray(v) for k, v in inputs.items()}
    f32 = _np.float32

    def rows(v):
        return _np.broadcast_to(v, (P, v.shape[-1]))

    def by_tf(v):
        return _np.concatenate([v] * 8, axis=0)

    def short(v):
        full = _np.zeros((P, v.shape[1]), f32)
        full[:v.shape[0]] = v
        return full

    u2 = a["L0_conv_U2"].T.reshape(2, P, 1, T)
    u2 = _np.broadcast_to(u2, (2, P, 8, T)).transpose(1, 0, 2, 3).reshape(P, 256)
    small = _np.concatenate([
        rows(a["L0_conv_U1"][None]), u2, by_tf(a["L0_conv_U3"][:, None]), by_tf(a["L0_conv_W3"][:, None]),
        by_tf(a["L0_conv_W2"]), short(a["L0_conv_W1"][:, None]), short(a["L0_conv_V_e"].T), short(a["L0_conv_b_e"][0].T),
        rows(a["L0_conv_tb"][None]), rows(a["L0_conv_rb"][None]), rows(a["L0_conv_gamma"][None]), rows(a["L0_conv_beta"][None]),
        a["L1_attn_bo"].reshape(2, P).T, a["L1_ffn_router_w"].T.reshape(2, P, 16).transpose(1, 0, 2).reshape(P, 32),
        rows(a["L1_ffn_correction_bias"][None])], axis=1)

    p = _np.arange(P)
    c = {
        "ident": p[:, None] == p[None], "mean8": (p[:, None] // 8 == p[None] // 8) / 8.0,
        "heads16": p[:, None] // 16 == p[None] // 16, "causal": p[:, None] <= p[None],
        "even": (p[:, None] // 16) % 2 == 0, "odd": (p[:, None] // 16) % 2 == 1,
        "halves": _np.concatenate([p[:, None] // 16 + 8 * h == _np.arange(16)[None] for h in range(2)], axis=1),
        "head": p[:, None] // 16 == _np.arange(8)[None], "diag8": p[:, None] // 16 == _np.arange(8)[None],
    }
    consts = _np.concatenate([c[n].astype(f32) for n in CONST], axis=1)
    spread = (_np.arange(32)[:, None] % 16 == _np.arange(1024)[None] // HIDDEN).astype(f32).reshape(32, ROUTED, P)
    theta = _np.concatenate([a["L0_conv_Theta"], a["L0_conv_rw"].T[None]], axis=0).transpose(1, 0, 2)
    tconv = a["L0_conv_tw"][:, :, 0, ::-1].transpose(1, 2, 0)
    given = {
        "x": a["x"], "small": small, "consts": consts, "spread_rows": spread, "cheb": a["L0_conv_cheb"], "theta": theta, "tconv": tconv,
        "vsT": a["L0_conv_V_s"].T, "bsT": a["L0_conv_b_s"][0].T,
        "wqkvT": _np.concatenate([a["L1_attn_Wq"].T, a["L1_attn_Wk"].T, a["L1_attn_Wv"].T], axis=1), "woT": a["L1_attn_Wo"].T,
        "gateT": _np.concatenate([a["L1_ffn_gate_w"].transpose(1, 0, 2).reshape(256, -1), a["L1_ffn_shared_gate_w"].T], axis=1),
        "upT": _np.concatenate([a["L1_ffn_up_w"].transpose(1, 0, 2).reshape(256, -1), a["L1_ffn_shared_up_w"].T], axis=1),
        "down": _np.concatenate([a["L1_ffn_down_w"].reshape(-1, 256), a["L1_ffn_shared_down_w"].T], axis=0),
    }
    nc = _bacc.Bacc("TRN2", target_bir_lowering=False, num_devices=1)
    arrays, args = {}, {}
    for name, v in given.items():
        v = _np.ascontiguousarray(v)
        arrays[f"in_{name}"] = v
        args[name] = nc.dram_tensor(f"in_{name}", v.shape, _mybir.dt.from_np(v.dtype), kind="ExternalInput").ap()
    args["out"] = nc.dram_tensor("out_x", a["x"].shape, F32, kind="ExternalOutput").ap()
    graph_attention_moe(nc, **args)
    r = _run(nc, [arrays], core_ids=[0])
    return r.results[0]["out_x"]
```

```python
import concourse.bass as bass
from concourse import mybir
from contextlib import ExitStack

F32 = mybir.dt.float32
F32R = mybir.dt.float32r
I32 = mybir.dt.int32
ALU = mybir.AluOpType
ACT = mybir.ActivationFunctionType
AX = mybir.AxisListType

P = 128
B = 16
N = 256
T = 16
L = 256
PAIRS = B // 2
HEADS = 16
EXPERTS = 16
HIDDEN = 64
SHARED = 512
FF = EXPERTS * HIDDEN + SHARED
CHUNKS = FF // P
ROUTED = EXPERTS * HIDDEN // P
NEWTON = 4
BIG = 3e30
UNCHOSEN = -1e30
FILLER = -2e30

SMALL = {}
CONST = {}


def columns(table, parts):
    at = 0
    for name, width in parts:
        table[name] = (at, at + width)
        at += width
    return at


N_SMALL = columns(SMALL, [("u1", 256), ("u2", 256), ("u3", 16), ("w3", 1), ("w2", 16), ("w1", 1), ("ve", 16),
                          ("be", 16), ("tb", 16), ("rb", 16), ("gamma", 16), ("beta", 16), ("bo", 2),
                          ("router", 32), ("corr", 16)])
N_CONST = columns(CONST, [("ident", 128), ("mean8", 128), ("heads16", 128), ("causal", 128), ("even", 1), ("odd", 1),
                          ("halves", 32), ("head", 8)])


class Signal:

    def __init__(self, sem, names, start=0):
        self.sem, self.names, self.start = sem, names, start
        self.turn = 0

    def at(self, pair, name):
        return pair * len(self.names) + self.names.index(name) + 1 + self.start

    def mark(self, name):
        assert self.names[self.turn % len(self.names)] == name, (name, self.names[self.turn % len(self.names)])
        self.turn += 1
        return self.sem, 1


BODY = """
    lg st0 y000 y001 y010 rt r1 +1 y011 y100 y101 y110 y111 r2 r3 r4 st1 o0 cb +2 o1 tc0 tc1 +2 z1 +3 xb z2 +4
    z3 +1 tok0 +3 gn tok1 +1 xg xT0 nrm xT1 +2 xl0 M xl1 prod k0 k1 v0 v1 Epre Eexp q0 +1 q1 kt Erep lr kv
    dent p2_0 p2_1 rd0 rd1 sp0 P0 s000 s001 +1 sp1 s002 +1 s003 +1 s010 +1 s011 +2 s012 s013 +1 at0 +1 P1 s100
    +1 s101 +2 s102 s103 +2 s110 s111 s112 +1 s113 at1 wo0 +7 wo1 tk0 tk1 +3 nrm2 +3 xn0 xn1 +3
""".split()
ROUTE_NAMES = ["lg", "rt", "r1", "r2", "r3", "r4", "cb"]
_NEXT = ["gn", "xg", "xT0", "xT1", "M", "prod", "Epre", "Eexp", "Erep", "lr", "p2_0", "p2_1", "sp0", "sp1"]
NEXT_NAMES = [n for n in BODY if n in _NEXT]
FRONT_NAMES = [n for n in BODY if n[0] != "+" and n not in ROUTE_NAMES + NEXT_NAMES]


def ffn_steps():
    steps = []
    for j in range(CHUNKS):
        steps += [("gu", j), ("h", j)]
        if j:
            steps.append(("dn", j - 1))
        steps.append(("w", j))
    return steps + [("dn", CHUNKS - 1), ("out", 0)]


def schedule():
    ffn = ffn_steps()
    out = []
    for name in BODY:
        if name[0] == "+":
            out += ffn[:int(name[1:])]
            ffn = ffn[int(name[1:]):]
        else:
            out.append(("route" if name in ROUTE_NAMES else "next" if name in NEXT_NAMES else "front", name))
    out += ffn
    assert out.index(("h", CHUNKS - 1)) < out.index(("front", "xn0"))
    return out


SCORES = [f"s{b}{lc}{j}" for b in range(2) for lc in range(2) for j in range(4)]
NO_TILE = ["xb", "xg", "Eexp", "z1", "z2", "z3", "nrm", "nrm2", "P0", "P1", "at0", "at1"]
TILES = [n for n in BODY if n[0] != "+" and n not in ROUTE_NAMES + NO_TILE]
RING = 3
SLOTS = -(-len(TILES) // RING) * RING


def graph_attention_moe(nc, x, out, small, consts, spread_rows, cheb, theta, tconv, vsT, bsT, wqkvT, woT, gateT, upT, down):
    x_v = x.rearrange("(p b) (c n) f t -> p b n c (f t)", b=2, n=P)
    out_v = out.rearrange("(p b) (c n) f t -> p b n c (f t)", b=2, n=P)
    with ExitStack() as ctx:
        def sb(name, shape, dt=F32):
            return ctx.enter_context(nc.sbuf_tensor(name, shape, dt))

        def sem(name):
            return ctx.enter_context(nc.semaphore(name))

        sm = sb("small_parameters", [P, N_SMALL])
        cs = sb("constants", [P, N_CONST])
        cheb_s = sb("cheb_s", [P, 3, 2, N])
        theta_s = sb("theta_s", [P, 4, 8, T])
        tconv_s = sb("tconv_s", [P, 10, T])
        vs_s = sb("vs_s", [P, 2, N])
        bs_s = sb("bs_s", [P, 2, N])
        ve_h = sb("ve_h", [T, 4, T])
        carrier = sb("carrier", [1, 2])
        iw1 = sb("iw1", [T, 18])
        biasy = sb("biasy", [P, T])
        wqkv_h = sb("wqkv_h", [P, 2, 768], F32R)
        wqkv_l = sb("wqkv_l", [P, 2, 768], F32R)
        wo_s = sb("wo_s", [P, 2, N])
        router_h = sb("router_h", [P, 2, P], F32R)
        router_l = sb("router_l", [P, 2, P], F32R)
        gate_h = sb("gate_h", [P, 2, FF], F32R)
        gate_l = sb("gate_l", [P, 2, FF], F32R)
        up_h = sb("up_h", [P, 2, FF], F32R)
        up_l = sb("up_l", [P, 2, FF], F32R)
        down_h = sb("down_h", [P, CHUNKS, N], F32R)
        down_l = sb("down_l", [P, CHUNKS, N], F32R)
        spread = sb("spread", [32, ROUTED, P], F32R)
        scratch = sb("scratch", [P, 3072])
        x2k = scratch[:, 0:1024].rearrange("p (c n) -> p c n", c=2)
        y_out = scratch[:, 1024:2048].rearrange("p (c n) -> p c n", c=2)
        sl = scratch[:, 2048:2560]
        hb = scratch[:, 2560:3072]

        def small_at(name, rows=P):
            a, b = SMALL[name]
            return sm[0:rows, a:b]

        def const_at(name, rows=P):
            a, b = CONST[name]
            return cs[0:rows, a:b]

        ident = const_at("ident")

        x_s = sb("x_s", [P, 2, 2, L])
        stats = sb("stats", [P, 4, 6])
        mv = sb("mv", [P, 4, 2])
        gmv = sb("gmv", [P, 4, 2])
        gsq = sb("gsq", [P, 4])
        gvar = sb("gvar", [P, 4])
        grstd = sb("grstd", [P, 4])
        lsum = sb("lsum", [P, 2, 2])
        lm = sb("lm", [P, 2, 2, T])
        m_s = sb("m_s", [P, 2 * T])
        te = sb("te", [T, 2, T])
        emax = sb("emax", [T, 2])
        esum = sb("esum", [T, 2])
        eT = sb("eT", [T, 2, T])
        eq = sb("eq", [T, 2, T])
        ab = sb("ab", [P, 4, 64])
        first = sb("first", [P, 3072])
        shared = sb("shared", [P, 9728])
        place = [0]

        def part(*shape):
            size = 1
            for s in shape:
                size *= s
            a = place[0]
            place[0] += size
            v = shared[:, a:a + size]
            names = "abcd"[:len(shape)]
            if len(shape) == 1:
                return v
            return v.rearrange(f"p ({' '.join(names)}) -> p {' '.join(names)}", **{n: s for n, s in zip(names, shape)})

        def quarter(a):
            return first[:, a:a + 1024].rearrange("p (b c n) -> p b c n", b=2, c=2)

        xg = quarter(0)
        xT = quarter(1024)
        sT = quarter(2048)
        th = xg
        a_s = [part(3, 2, N), part(3, 2, N)]
        y_s = part(2, 2, 2, 384)
        resb = part(2, 2, 256)
        sg, z, zsq = xg, xT, sT
        zg = sg
        junk = sT[:, 0, 0, :]
        um = first[:, 2560:3072]
        eTx = first[0:T, 2048:2560].rearrange("p (b j f) -> p b j f", b=2, j=T)
        r2 = first[0:T, 2048:2560]
        l2 = first[0:T, 2560:3072]
        conv_end = place[0]
        place[0] = 0
        xt = part(2, 2, N)
        e_s = part(2, 512)
        k_f = part(2, 512)
        q_f = part(2, 512)
        q_e = part(2, 512)
        q_o = part(2, 512)
        ktok = part(512)
        kvm = part(512)
        zs = part(2, 512)
        rd_s = xt.rearrange("p b c n -> p b (c n)")
        attn = e_s
        rdx = zs.rearrange("p c n -> p (c n)").rearrange("p (q h e) -> p q h e", q=4, h=HEADS)
        p_s = part(3, 512)
        assert max(place[0], conv_end) <= 9728, (place[0], conv_end)

        smax = sb("smax", [P, 2, 2])
        ssum = sb("ssum", [P, 2, 2])
        rinv = sb("rinv", [P, 2, 2])
        msum = sb("msum", [P, 2, 32])
        vsum = sb("vsum", [P, 2, 32])
        vrstd = sb("vrstd", [P, 2, 32])
        x1 = sb("x1", [P, 2, 2, L])
        tst = sb("tst", [P, 4, 6])
        tmv = sb("tmv", [P, 4, 2])
        tve = sb("tve", [P, 4])
        trs = sb("trs", [P, 4])
        xa_h = sb("xa_h", [P, 2, 512], F32R)
        xa_l = sb("xa_l", [P, 2, 512], F32R)
        v_s = sb("v_s", [P, 2, 2, 8, 48])
        minus_half = sb("minus_half", [P, 4])
        one = sb("one", [P, 1])
        rd = sb("rd", [P, 4, HEADS])
        x2 = x1[:, :, :, :].rearrange("p c b l -> p c (b l)")
        xf_h = sb("xf_h", [P, 2, 512], F32R)
        xf_l = sb("xf_l", [P, 2, 512], F32R)
        lgT = k_f[0:EXPERTS, 0, :]
        sc = sb("sc", [P, 4, EXPERTS])
        scb = sb("scb", [P, 4, EXPERTS])
        pairs = sb("pairs", [P, 16, 6])
        gs = sb("gs", [P, 4, 10])
        gtop = sb("gtop", [P, 4, 8])
        gtake = sb("gtake", [P, 4, 8])
        gmark = sb("gmark", [P, 4, 10])
        gneg = sb("gneg", [P, 4, 4])
        es = sb("es", [P, 4, 20])
        etop = sb("etop", [P, 4, 8])
        etake = sb("etake", [P, 4, 8])
        emark = sb("emark", [P, 4, 20])
        wsel = sb("wsel", [P, 4, EXPERTS])
        wsum = sb("wsum", [P, 4])
        whl = sb("whl", [P, 4, 2, EXPERTS], F32R)
        comb = sb("comb", [32, 512], F32R)
        hh = sb("hh", [P, 2, 512], F32R)
        hl = sb("hl", [P, 2, 512], F32R)

        bank = [ctx.enter_context(nc.psum_tensor(f"ring{i}", [P, 512], F32)) for i in range(RING)]
        num = ctx.enter_context(nc.psum_tensor("num", [P, 512], F32))
        g_ps = ctx.enter_context(nc.psum_tensor("g_ps", [P, 512], F32))
        u_ps = ctx.enter_context(nc.psum_tensor("u_ps", [P, 512], F32))
        d_ps = [ctx.enter_context(nc.psum_tensor(f"d_ps{m}", [P, 512], F32)) for m in range(2)]

        def tile(name):
            return bank[TILES.index(name) % RING]

        load = {n: sem("load_" + n) for n in ("small", "graph", "blocks")}
        x_loaded = sem("x_loaded")
        piece_loaded = [sem(f"piece_loaded{i}") for i in range(2)]
        piece_high = sem("piece_high")
        piece_low = sem("piece_low")
        out_stored = sem("out_stored")
        prep_dve = sem("prep_dve")
        prep_act = sem("prep_act")
        prep_pool = sem("prep_pool")
        prep_pe = sem("prep_pe")
        BI = ["0", "1"]
        filled_front = Signal(sem("front_tile_filled"), [n for n in TILES if n not in NEXT_NAMES])
        filled_next = Signal(sem("next_tile_filled"), [n for n in TILES if n in NEXT_NAMES])

        def filled(name):
            return filled_next if name in NEXT_NAMES else filled_front

        def in_order(results):
            return [r for name in NEXT_NAMES + FRONT_NAMES for r in results.get(name, "").split()]

        conv_dve = Signal(sem("conv_by_dve"), in_order({
            "gn": "bn0 bn1 bn2 bn3 ag0 ag1 ag2 ag3 msq m2 gm gsq gvar", "xg": "xg0 xg1 xg2 xg3", "xT1": "L00 L01 L10 L11 Lm",
            "M": "um M", "prod": "te", "Epre": "emax esub", "Eexp": "e1 e2 e3 e4 e5 esum erec ET", "Erep": "EW WE", "p2_0": "pb0", "p2_1": "pb1",
            "sp0": "smax0", "sp1": "smax1", **{n: n for n in FRONT_NAMES if n[0] == "y"}, "st0": "rinv0 A00 A01 A02",
            "st1": "rinv1 A10 A11 A12", "tc0": "z00 z01", "tc1": "z10 z11", "z1": "sum0 sum1 mean sub0 sub1 zg0 zg1",
            "z2": "vs0 vs1 vv half guess " + " ".join(f"yy{i} yv{i} y{i}" for i in range(NEWTON)), "z3": "n10 n30 n11 n31"}))
        conv_act = Signal(sem("conv_by_act"), in_order({
            "xT0": "xT0", "xT1": "xT1", **{n: n for n in FRONT_NAMES if n[0] == "y"}, "prod": "thE", "Epre": "expE", "lr": "l2 r2",
            "p2_0": "th0", "p2_1": "th1", "sp0": "ex00 ex01", "sp1": "ex10 ex11", "o0": "sg0", "o1": "sg1", "tc0": "relu0", "tc1": "relu1",
            "z1": "sq0 sq1"}))
        conv_pool = Signal(sem("conv_by_pool"), ["rstd", "xb0", "xb1"])
        norm_names = [f"bs{q}" for q in range(4)] + [f"ba{q}" for q in range(4)] + ["ve"] + [f"nm{q}" for q in range(4)] + ["lo0", "lo1"]
        attn_dve = Signal(sem("attn_by_dve"), in_order({
            "tok0": "bs0 bs1", "tok1": "bs2 bs3 ba0 ba1 ba2 ba3 ve", "nrm": "nm0 nm1 nm2 nm3", "xl0": "lo0", "xl1": "lo1", "k0": "kmin0 k0",
            "k1": "kmin1 k1 scan00 scan01 scan10 scan11", "q0": "qmin0 q0 zq0", "q1": "qmin1 q1 zq1", "kv": "kvm", "dent": "da dr",
            **{n: n for n in SCORES}, "at0": "at0", "at1": "at1", "wo0": "x20", "wo1": "x21"}))
        attn_act = Signal(sem("attn_by_act"), in_order({
            "xl0": "hi0", "xl1": "hi1", "k0": "ek0", "k1": "ek1", "v0": "ve0 vo0", "v1": "ve1 vo1", "q0": "eq0", "q1": "eq1 qe0 qo0 qe1 qo1",
            "kt": "kt", "dent": "rdx", "rd0": "rd0", "rd1": "rd1"}))
        attn_pool = Signal(sem("attn_by_pool"), ["rstd"])
        route_dve = Signal(sem("route_by_dve"), norm_names + [
            "one", "sig", "sb", "p1", "p2", "p3", "gs"] + [f"gx{q}" for q in range(4)] + ["gt"] + [f"gr{q}" for q in range(4)]
            + ["gn", "es"] + [f"ex{q}" for q in range(4)] + ["et"] + [f"er{q}" for q in range(4)]
            + ["ws", "wsum", "weps", "wrec", "wn", "wh", "wl"])
        route_act = Signal(sem("route_by_act"), ["hi0", "hi1", "lg", "eneg", "cb"])
        route_pool = Signal(sem("route_by_pool"), ["rstd"])
        route_pe = Signal(sem("route_by_pe"), ["lg", "rt", "cb"])
        pv_done = Signal(sem("pv_by_pe"), SCORES)
        fp = []
        for k, j in ffn_steps():
            fp += {"gu": [f"g{j}", f"u{j}"], "h": [f"cm{j}"] if j < ROUTED else [], "dn": [f"dn{j}"]}.get(k, [])
        ffn_pe = Signal(sem("ffn_by_pe"), fp)
        fd = []
        fa = []
        for k, j in ffn_steps():
            if k == "h":
                fd.append(f"h{j}")
                fa.append(f"si{j}")
            if k == "w":
                fd += [f"w{j}", f"lo{j}"] if j < ROUTED else [f"lo{j}"]
                fa.append(f"hi{j}")
            if k == "out":
                fd += ["out0", "out1"]
        ffn_dve = Signal(sem("ffn_by_dve"), fd, start=1)
        ffn_act = Signal(sem("ffn_by_act"), fa)
        x2_kept = Signal(sem("x2_kept_by_pool"), ["x2k"])

        READ_OUT = {"gn": [(conv_dve, "gm")], "M": [(conv_dve, "um")], "prod": [(conv_dve, "te")],
                    "Epre": [(conv_dve, "esub")], "Erep": [(conv_dve, "WE")], "lr": [(conv_act, "r2")],
                    "kt": [(attn_act, "kt")], "kv": [(attn_dve, "kvm")], "dent": [(attn_dve, "da")]}
        for b in BI:
            READ_OUT["xT" + b] = [(conv_act, "xT" + b)]
            READ_OUT["p2_" + b] = [(conv_dve, "pb" + b)]
            READ_OUT["sp" + b] = [(conv_act, f"ex{b}1")]
            READ_OUT["st" + b] = [(conv_dve, f"A{b}2")]
            READ_OUT["o" + b] = [(conv_act, "sg" + b)]
            READ_OUT["tc" + b] = [(conv_dve, f"z{b}1")]
            READ_OUT["tok" + b] = [(attn_dve, f"nm{2 * int(b) + 1}")]
            READ_OUT["tk" + b] = [(route_dve, f"nm{2 * int(b) + 1}")]
            READ_OUT["xl" + b] = [(attn_dve, "lo" + b)]
            READ_OUT["xn" + b] = [(route_dve, "lo" + b)]
            READ_OUT["q" + b] = [(attn_dve, "q" + b)]
            READ_OUT["k" + b] = [(attn_dve, "k" + b)]
            READ_OUT["v" + b] = [(attn_act, "vo" + b)]
            READ_OUT["rd" + b] = [(attn_act, "rd" + b)]
            READ_OUT["wo" + b] = [(attn_dve, "x2" + b)]
            for m in BI:
                for c in BI:
                    READ_OUT["y" + b + m + c] = [(conv_act, "y" + b + m + c), (conv_dve, "y" + b + m + c)]
        for n in SCORES:
            READ_OUT[n] = [(attn_dve, n)]

        def wait_bank(eng, p, name):
            slot = TILES.index(name)
            turn = p - 1 if name in NEXT_NAMES else p
            while True:
                slot -= RING
                if slot < 0:
                    slot += SLOTS
                    turn = turn - 1
                if isinstance(turn, int) and turn < -1:
                    return
                if slot >= len(TILES):
                    continue
                if TILES[slot] in NEXT_NAMES:
                    if isinstance(turn, int) and turn + 1 >= PAIRS:
                        continue
                    turn = turn + 1
                elif isinstance(turn, int) and turn < 0:
                    continue
                break
            for signal, result in READ_OUT[TILES[slot]]:
                eng.wait_ge(signal.sem, signal.at(turn, result))

        def carry(dve):
            dve.memset(carrier[:, 0:1], 0.0)

        def mm3(eng, ps, wh, wl, xh, xl, start, stop):
            eng.matmul(ps, wh, xh, start=start, stop=False)
            eng.matmul(ps, wh, xl, start=False, stop=False)
            return eng.matmul(ps, wl, xh, start=False, stop=stop)

        def run(body):
            eng, front, route, ffn = body

            def step(p, kind, what):
                if kind == "front":
                    front(p, what)
                elif kind == "next":
                    front(p + 1, what)
                elif kind == "route":
                    route(p - 1, what)
                else:
                    ffn(p - 1, kind, what)

            for name in NEXT_NAMES:
                front(0, name)
            for kind, what in schedule():
                if kind in ("front", "next"):
                    step(0, kind, what)
            with eng.Fori(1, PAIRS - 1) as p:
                for kind, what in schedule():
                    step(p, kind, what)
            for kind, what in schedule():
                if kind != "next":
                    step(PAIRS - 1, kind, what)
            for kind, what in schedule():
                if kind not in ("front", "next"):
                    step(PAIRS, kind, what)

        PIECES = [(wqkvT.rearrange("(c j) k -> j c k", j=P), wqkv_h[:, :, :], wqkv_l[:, :, :])]
        for w, high, low in ((gateT, gate_h, gate_l), (upT, up_h, up_l)):
            PIECES += [(w[k * P:(k + 1) * P, :], high[:, k, :], low[:, k, :]) for k in range(2)]
        for k in range(2):
            half = slice(k * CHUNKS // 2, (k + 1) * CHUNKS // 2)
            PIECES.append((down[k * FF // 2:(k + 1) * FF // 2, :].rearrange("(c j) n -> j c n", j=P), down_h[:, half, :], down_l[:, half, :]))
        PIECES.append((spread_rows, spread[:, :, :], None))
        SPLIT_AT = ["sp1", "rd1", "s001", "s003", "s011", "s101", "s103", "s111"]

        def piece(i):
            if i == len(PIECES) - 1:
                return scratch[0:32, 1536 * (i % 2):1536 * (i % 2) + 1024].rearrange("p (j m) -> p j m", m=P)
            v = scratch[:, 1536 * (i % 2):1536 * (i % 2) + 1536]
            c = {0: 2, 5: CHUNKS // 2, 6: CHUNKS // 2}.get(i)
            return v.rearrange("p (c n) -> p c n", c=c) if c else v

        block = ctx.enter_context(nc.Block())

        @block.sync
        def _(sp):
            for b in range(2):
                sp.dma_start(x_s[:, b], x_v[0, b]).then_inc(x_loaded, 16)
            sp.dma_start(cs[:, :], consts).then_inc(load["small"], 16)
            sp.dma_start(sm[:, :], small).then_inc(load["small"], 16)
            sp.wait_ge(prep_pool, 2)
            for t in range(8):
                rows = slice(16 * t, 16 * t + 16)
                sp.dma_start(theta_s[rows, :, t, :], theta).then_inc(load["blocks"], 16)
                sp.dma_start(tconv_s[rows, t:t + 3, :], tconv).then_inc(load["blocks"], 16)
            sp.dma_start(vs_s[:, :, :], vsT.rearrange("(c j) k -> j c k", j=P)).then_inc(load["graph"], 16)
            sp.dma_start(bs_s[:, :, :], bsT.rearrange("(c j) k -> j c k", j=P)).then_inc(load["graph"], 16)
            for k in range(3):
                sp.dma_start(cheb_s[:, k], cheb[k].rearrange("(c m) n -> m c n", m=P)).then_inc(load["graph"], 16)
            sp.dma_start(wo_s[:, :, :], woT.rearrange("(c j) k -> j c k", j=P)).then_inc(load["graph"], 16)
            def load_piece(i):
                if i >= 2:
                    sp.wait_ge(piece_low, i - 1)
                sp.dma_start(piece(i), PIECES[i][0]).then_inc(piece_loaded[i % 2], 16)

            for i in range(3):
                load_piece(i)

            def prefetch(p, next_pair):
                sp.wait_ge(conv_pool.sem, conv_pool.at(p, "xb1"))
                for b in range(2):
                    sp.dma_start(x_s[:, b], x_v[next_pair, b]).then_inc(x_loaded, 16)

            def store(p):
                sp.wait_ge(ffn_dve.sem, ffn_dve.at(p, "out1"))
                for b in range(2):
                    sp.dma_start(out_v[p, b], y_out[:, :, b * L:(b + 1) * L]).then_inc(out_stored, 16)
            prefetch(0, 1)
            for i in range(3, len(PIECES)):
                load_piece(i)
            with sp.Fori(1, PAIRS - 1) as p:
                prefetch(p, p + 1)
                store(p - 1)
            store(PAIRS - 2)
            store(PAIRS - 1)
            sp.wait_ge(out_stored, 32 * PAIRS + 32)

        @block.gpsimd
        def _(pool):
            pool.memset(theta_s[:, :, :, :], 0.0).then_inc(prep_pool, 1)
            pool.memset(tconv_s[:, :, :], 0.0).then_inc(prep_pool, 1)
            pool.memset(minus_half[:, :], -0.5).then_inc(prep_pool, 1)
            pool.memset(one[:, :], 1.0).then_inc(prep_pool, 1)
            pool.memset(ab[:, :, :], 0.0).then_inc(prep_pool, 1)
            pool.memset(v_s[:, :, :, :, :], 0.0).then_inc(prep_pool, 1)
            pool.memset(gs[:, :, :], FILLER).then_inc(prep_pool, 1)
            pool.memset(gtake[:, :, :], FILLER).then_inc(prep_pool, 1)
            pool.memset(es[:, :, :], FILLER).then_inc(prep_pool, 1)
            pool.memset(etake[:, :, :], FILLER).then_inc(prep_pool, 1)
            pool.wait_ge(prep_pool, 4)
            pool.wait_ge(load["small"], 32)

            def front(p, name):
                if name == "gn":
                    pool.wait_ge(conv_dve.sem, conv_dve.at(p, "gvar"))
                    pool.tensor_tensor(grstd[:, :], gvar[:, :], minus_half[:, 0:4], ALU.pow).then_inc(*conv_pool.mark("rstd"))
                if name == "xb":
                    pool.wait_ge(conv_dve.sem, conv_dve.at(p, "xg3"))
                    if not (isinstance(p, int) and p == 0):
                        pool.wait_ge(filled("tk1").sem, filled("tk1").at(p - 1, "tk1"))
                        pool.wait_ge(x2_kept.sem, x2_kept.at(p - 1, "x2k"))
                    beta = small_at("beta").unsqueeze(1).to_broadcast([P, 2, T]).unsqueeze(2).to_broadcast([P, 2, T, T])
                    for b in range(2):
                        pool.tensor_tensor(x1[:, :, b, :].rearrange("p m (f t) -> p m f t", t=T), x_s[:, b].rearrange("p m (f t) -> p m f t", t=T),
                                           beta, ALU.add).then_inc(*conv_pool.mark(f"xb{b}"))
                if name == "tok1":
                    pool.wait_ge(attn_dve.sem, attn_dve.at(p, "ve"))
                    pool.tensor_tensor(trs[:, :], tve[:, :], minus_half[:, 0:4], ALU.pow).then_inc(*attn_pool.mark("rstd"))
                if name == "tk1":
                    pool.wait_ge(route_dve.sem, route_dve.at(p, "ve"))
                    pool.tensor_tensor(trs[:, :], tve[:, :], minus_half[:, 0:4], ALU.pow).then_inc(*route_pool.mark("rstd"))

            def ffn(p, kind, j):
                if (kind, j) == ("gu", 0):
                    pool.wait_ge(attn_dve.sem, attn_dve.at(p, "x21"))
                    pool.wait_ge(ffn_dve.sem, ffn_dve.at(p, "h0") - 1)
                    pool.tensor_tensor(x2k[:, :, :], x2[:, :, :], one[:, 0:1].unsqueeze(1).to_broadcast([P, 2, 512]), ALU.mult).then_inc(*x2_kept.mark("x2k"))

            run((pool, front, lambda p, name: None, ffn))

        @block.scalar
        def _(act):
            act.wait_ge(load["small"], 32)
            act.wait_ge(prep_dve, 1)
            act.activation(router_h[:, :, 0:16], small_at("router").rearrange("p (c e) -> p c e", c=2), ACT.Copy).then_inc(prep_act, 1)

            def split(i):
                act.wait_ge(piece_loaded[i % 2], 16 * (i // 2 + 1))
                act.activation(PIECES[i][1], piece(i), ACT.Copy).then_inc(piece_high, 1)

            def heads(ps, c):
                return ps.rearrange("p (lc j e) -> p (lc j) e", lc=2, e=32)[:, :, 16 * c:16 * c + 16]

            def front(p, name):
                t = tile(name) if name in TILES else None
                if name in TILES:
                    act_reads = name[:2] in ("xT", "y0", "y1", "lr", "sp", "xl", "xn", "rd", "lg", "rt", "cb", "kt") or name in (
                        "Epre", "o0", "o1", "q0", "q1", "k0", "k1", "v0", "v1")
                    if act_reads and name != "Epre" and name[:2] != "sp":
                        act.wait_ge(filled(name).sem, filled(name).at(p, name))
                if name in ("xT0", "xT1"):
                    b = int(name[2])
                    act.activation(xT[:, b].rearrange("p c n -> p (c n)"), t[:, :], ACT.Copy).then_inc(*conv_act.mark(name))
                if name[0] == "y":
                    b, m, c = map(int, name[1:])
                    act.activation(y_s[:, b, m, c, :], t[:, 0:384], ACT.Copy).then_inc(*conv_act.mark(name))
                if name == "prod":
                    act.wait_ge(conv_dve.sem, conv_dve.at(p, "te"))
                    act.activation(te[:, :, :], te[:, :, :], ACT.Tanh, scale=0.5).then_inc(*conv_act.mark("thE"))
                if name == "Epre":
                    act.wait_ge(conv_dve.sem, conv_dve.at(p, "esub"))
                    act.activation(eT[:, :, :], eT[:, :, :], ACT.Tanh, scale=0.125).then_inc(*conv_act.mark("expE"))
                if name == "lr":
                    act.activation(l2[:, :], t[0:16, :], ACT.Copy).then_inc(*conv_act.mark("l2"))
                    act.activation(r2[:, :], t[32:48, :], ACT.Copy).then_inc(*conv_act.mark("r2"))
                if name in ("p2_0", "p2_1"):
                    b = int(name[3])
                    act.wait_ge(conv_dve.sem, conv_dve.at(p, f"pb{b}"))
                    act.activation(th[:, b], th[:, b], ACT.Tanh, scale=0.5).then_inc(*conv_act.mark(f"th{b}"))
                if name in ("sp0", "sp1"):
                    b = int(name[2])
                    act.wait_ge(conv_dve.sem, conv_dve.at(p, f"smax{b}"))
                    for kc in range(2):
                        act.activation(sT[:, b, kc, :], t[:, kc * N:(kc + 1) * N], ACT.Exp, bias=smax[:, b, kc:kc + 1],
                                       accum_out=ssum[:, b, kc:kc + 1]).then_inc(*conv_act.mark(f"ex{b}{kc}"))
                if name in ("o0", "o1"):
                    b = int(name[1])
                    act.activation(sg[:, b].rearrange("p c n -> p (c n)"), t[:, :], ACT.Relu).then_inc(*conv_act.mark(f"sg{b}"))
                if name in ("tc0", "tc1"):
                    b = int(name[2])
                    act.wait_ge(conv_dve.sem, conv_dve.at(p, f"z{b}1"))
                    act.activation(z[:, b], z[:, b], ACT.Relu).then_inc(*conv_act.mark(f"relu{b}"))
                if name == "z1":
                    for b in range(2):
                        act.wait_ge(conv_dve.sem, conv_dve.at(p, f"sub{b}"))
                        act.activation(zsq[:, b], z[:, b], ACT.Square).then_inc(*conv_act.mark(f"sq{b}"))
                if name in ("xl0", "xl1"):
                    c = int(name[2])
                    act.activation(xa_h[:, c, :], t[:, :], ACT.Copy).then_inc(*attn_act.mark(f"hi{c}"))
                if name in ("k0", "k1", "q0", "q1"):
                    c = int(name[1])
                    if name[0] == "q":
                        act.wait_ge(attn_dve.sem, attn_dve.at(p, f"k{c}"))
                    act.activation(e_s[:, c, :], t[:, :], ACT.Exp).then_inc(*attn_act.mark("e" + name))
                if name == "q1":
                    for c in range(2):
                        act.wait_ge(attn_dve.sem, attn_dve.at(p, f"q{c}"))
                        act.activation(q_e[:, c, :], q_f[:, c, :], ACT.Copy, scale=const_at("even")).then_inc(*attn_act.mark(f"qe{c}"))
                        act.activation(q_o[:, c, :], q_f[:, c, :], ACT.Copy, scale=const_at("odd")).then_inc(*attn_act.mark(f"qo{c}"))
                if name in ("v0", "v1"):
                    b = int(name[1])
                    act.activation(v_s[:, b].rearrange("p c j e -> p (c j) e")[:, :, 0:16], heads(t[:, :], 0), ACT.Copy).then_inc(*attn_act.mark(f"ve{b}"))
                    act.activation(v_s[:, b].rearrange("p c j e -> p (c j) e")[:, :, 32:48], heads(t[:, :], 1), ACT.Copy).then_inc(*attn_act.mark(f"vo{b}"))
                if name == "kt":
                    act.activation(ktok[:, :], t[:, :], ACT.Copy).then_inc(*attn_act.mark("kt"))
                if name == "dent":
                    act.wait_ge(attn_dve.sem, attn_dve.at(p, "dr"))
                    act.activation(rdx.rearrange("p q h e -> p (q h) e"), rd[:, :, :].rearrange("p q h -> p (q h)").unsqueeze(2).to_broadcast([P, 64, T]),
                                   ACT.Copy).then_inc(*attn_act.mark("rdx"))
                if name in ("rd0", "rd1"):
                    c = int(name[2])
                    act.activation(rd_s[:, c, :], t[:, :], ACT.Copy).then_inc(*attn_act.mark(name))
                if name in ("xn0", "xn1"):
                    c = int(name[2])
                    act.activation(xf_h[:, c, :], t[:, :], ACT.Copy).then_inc(*route_act.mark(f"hi{c}"))
                if isinstance(p, int) and p == 0 and name in SPLIT_AT:
                    split(SPLIT_AT.index(name))

            def route(p, name):
                if name in ("lg", "rt", "cb"):
                    act.wait_ge(route_pe.sem, route_pe.at(p, name))
                t = num
                if name == "lg":
                    act.activation(lgT[:, :], t[0:EXPERTS, :], ACT.Copy).then_inc(*route_act.mark("lg"))
                if name == "rt":
                    act.activation(sc[:, :, :].rearrange("p q e -> p (q e)"), t[:, 0:64], ACT.Exp, scale=-1.0).then_inc(*route_act.mark("eneg"))
                if name == "cb":
                    act.activation(comb[:, :], t[0:32, :], ACT.Copy).then_inc(*route_act.mark("cb"))

            def ffn(p, kind, j):
                if kind == "h":
                    act.wait_ge(ffn_pe.sem, ffn_pe.at(p, f"g{j}"))
                    act.activation(sl, g_ps[:, :], ACT.Silu).then_inc(*ffn_act.mark(f"si{j}"))
                if kind == "w":
                    act.wait_ge(ffn_dve.sem, ffn_dve.at(p, f"w{j}" if j < ROUTED else f"h{j}"))
                    act.activation(hh[:, j % 2, :], hb, ACT.Copy).then_inc(*ffn_act.mark(f"hi{j}"))

            run((act, front, route, ffn))

        @block.vector
        def _(dve):
            dve.memset(carrier[:, 0:1], 0.0).then_inc(ffn_dve.sem, 1)
            dve.memset(carrier[:, 1:2], 0.0).then_inc(out_stored, 32)
            dve.memset(router_h[:, :, :].bitcast(F32), 0.0).then_inc(prep_dve, 1)
            dve.memset(router_l[:, :, :].bitcast(F32), 0.0).then_inc(prep_dve, 1)
            dve.wait_ge(load["small"], 32)
            dve.tensor_scalar(ve_h[:, :, :], small_at("ve", T).unsqueeze(1).to_broadcast([T, 4, T]), 0.5, None, ALU.mult).then_inc(prep_dve, 1)
            dve.tensor_copy(iw1[:, 0:16], const_at("ident", T)[:, 0:16]).then_inc(prep_dve, 1)
            dve.tensor_copy(iw1[:, 16:17], small_at("w1", T)).then_inc(prep_dve, 1)
            dve.tensor_copy(iw1[:, 17:18], small_at("w1", T)).then_inc(prep_dve, 1)
            dve.tensor_tensor(biasy[:, :], small_at("tb"), small_at("rb"), ALU.add).then_inc(prep_dve, 1)
            dve.wait_ge(prep_act, 1)
            dve.wait_ge(prep_dve, 2)
            dve.tensor_tensor(router_l[:, :, 0:16], small_at("router").rearrange("p (c e) -> p c e", c=2),
                              router_h[:, :, 0:16].bitcast(F32), ALU.subtract).then_inc(prep_dve, 1)
            dve.wait_ge(prep_dve, 8)
            dve.wait_ge(prep_pool, 10)

            def split(i):
                _, high, low = PIECES[i]
                if low is not None:
                    dve.wait_ge(piece_high, i + 1)
                    dve.tensor_tensor(low, piece(i), high.bitcast(F32), ALU.subtract).then_inc(piece_low, 1)

            def layer_stats(p, sig, t, b):
                for lc in range(2):
                    q = 2 * b + lc
                    dve.bn_stats(tst[:, q, :], t[:, lc * N:(lc + 1) * N]).then_inc(*sig.mark(f"bs{q}"))

            def gather_stats(p, sig):
                dve.wait_ge(sig.sem, sig.at(p, "bs3"))
                carry(dve)
                for q in range(4):
                    dve.bn_aggr(tmv[:, q, :], tst[:, q, :]).then_inc(*sig.mark(f"ba{q}"))
                dve.wait_ge(sig.sem, sig.at(p, "ba3"))
                dve.tensor_scalar(tve[:, :], tmv[:, :, 1], 1e-5, None, ALU.add).then_inc(*sig.mark("ve"))

            def apply_norm(p, sig, pool_sig, tiles):
                dve.wait_ge(pool_sig.sem, pool_sig.at(p, "rstd"))
                for q in range(4):
                    dve.tensor_scalar(xt[:, q // 2, q % 2, :], tile(tiles[q // 2])[:, (q % 2) * N:(q % 2 + 1) * N],
                                      tmv[:, q, 0:1], trs[:, q:q + 1], ALU.subtract, ALU.mult).then_inc(*sig.mark(f"nm{q}"))

            def by_time(v):
                return v.rearrange("p m (t o) -> p m o t", o=T)

            def per_row(v):
                return v.rearrange("p (m o) -> p m o", m=2).unsqueeze(2).to_broadcast([P, 2, T, T])

            def own(sig, p, name):
                dve.wait_ge(sig.sem, sig.at(p, name))

            def front(p, name):
                cv, at, rt = conv_dve, attn_dve, route_dve
                t = tile(name) if name in TILES else None
                if name in ("M", "prod", "Epre", "Erep", "p2_0", "p2_1", "sp0", "sp1", "tc0", "tc1", "tok0", "tok1", "xl0", "xl1",
                            "k0", "k1", "q0", "q1", "kv", "dent", "wo0", "wo1", "tk0", "tk1", "xn0", "xn1") or name[0] == "y":
                    dve.wait_ge(filled(name).sem, filled(name).at(p, name))
                if name == "gn":
                    dve.wait_ge(x_loaded, 32 * p + 32)
                    for q in range(4):
                        dve.bn_stats(stats[:, q, :], x_s[:, q // 2, q % 2, :]).then_inc(*cv.mark(f"bn{q}"))
                    own(cv, p, "bn3")
                    carry(dve)
                    for q in range(4):
                        dve.bn_aggr(mv[:, q, :], stats[:, q, :]).then_inc(*cv.mark(f"ag{q}"))
                    own(cv, p, "ag3")
                    dve.tensor_tensor(gsq[:, :], mv[:, :, 0], mv[:, :, 0], ALU.mult).then_inc(*cv.mark("msq"))
                    own(cv, p, "msq")
                    dve.tensor_tensor(mv[:, :, 1], mv[:, :, 1], gsq[:, :], ALU.add).then_inc(*cv.mark("m2"))
                    dve.wait_ge(filled("gn").sem, filled("gn").at(p, "gn"))
                    dve.tensor_copy(gmv[:, :, :].rearrange("p q s -> p (q s)"), t[:, 0:8]).then_inc(*cv.mark("gm"))
                    own(cv, p, "gm")
                    dve.tensor_tensor(gsq[:, :], gmv[:, :, 0], gmv[:, :, 0], ALU.mult).then_inc(*cv.mark("gsq"))
                    own(cv, p, "gsq")
                    dve.scalar_tensor_tensor(gvar[:, :], gmv[:, :, 1], 1e-5, gsq[:, :], ALU.add, ALU.subtract).then_inc(*cv.mark("gvar"))
                if name == "xg":
                    dve.wait_ge(conv_pool.sem, conv_pool.at(p, "rstd"))
                    for q in range(4):
                        dve.tensor_scalar(xg[:, q // 2, q % 2, :].rearrange("p (t f) -> p t f", t=T),
                                          x_s[:, q // 2, q % 2, :].rearrange("p (f t) -> p t f", t=T), gmv[:, q, 0:1], grstd[:, q:q + 1],
                                          ALU.subtract, ALU.mult).then_inc(*cv.mark(f"xg{q}"))
                if name == "xT1":
                    for b in range(2):
                        dve.wait_ge(conv_act.sem, conv_act.at(p, f"xT{b}"))
                        for c in range(2):
                            if b or c:
                                own(cv, p, ["L00", "L01", "L10"][2 * b + c - 1])
                            dve.tensor_tensor_reduce(junk[:, :], xT[:, b, c, :], small_at("u1"), 1.0, 0.0, ALU.mult, ALU.add,
                                                     lsum[:, b, c:c + 1]).then_inc(*cv.mark(f"L{b}{c}"))
                    own(cv, p, "L11")
                    dve.tensor_tensor(lm[:, :, :, :], const_at("halves").rearrange("p (c t) -> p c t", c=2).unsqueeze(1).to_broadcast([P, 2, 2, T]),
                                      lsum[:, :, :].unsqueeze(3).to_broadcast([P, 2, 2, T]), ALU.mult).then_inc(*cv.mark("Lm"))
                if name == "M":
                    dve.tensor_tensor(um[:, :].rearrange("p (s f) -> p s f", f=T), t[:, :].rearrange("p (s f) -> p s f", f=T),
                                      small_at("u3").unsqueeze(1).to_broadcast([P, 2 * T, T]), ALU.mult).then_inc(*cv.mark("um"))
                    own(cv, p, "um")
                    dve.tensor_reduce(m_s[:, :], um[:, :].rearrange("p (s f) -> p s f", f=T), AX.X, ALU.add).then_inc(*cv.mark("M"))
                if name[0] == "y":
                    b, m, c = map(int, name[1:])
                    dve.wait_ge(conv_act.sem, conv_act.at(p, name))
                    dve.tensor_tensor(resb[:, b, m, c * P:(c + 1) * P].rearrange("p (t o) -> p t o", o=T),
                                      t[:, 384:512].rearrange("p (t o) -> p t o", o=T),
                                      biasy[:, :].unsqueeze(1).to_broadcast([P, 8, T]), ALU.add).then_inc(*cv.mark(name))
                if name == "prod":
                    dve.tensor_tensor(te[:, :, :], t[0:T, 0:32].rearrange("p (b s) -> p b s", b=2),
                                      small_at("be", T).unsqueeze(1).to_broadcast([T, 2, T]), ALU.add).then_inc(*cv.mark("te"))
                if name == "Epre":
                    e = t[0:T, 0:32].rearrange("p (b s) -> p b s", b=2)
                    dve.tensor_reduce(emax[:, :], e, AX.X, ALU.max).then_inc(*cv.mark("emax"))
                    own(cv, p, "emax")
                    dve.tensor_tensor(eT[:, :, :], e, emax[:, :].unsqueeze(2).to_broadcast([T, 2, T]), ALU.subtract).then_inc(*cv.mark("esub"))
                if name == "Eexp":
                    dve.wait_ge(conv_act.sem, conv_act.at(p, "expE"))
                    dve.tensor_scalar(eq[:, :, :], eT[:, :, :], -1.0, 1.0, ALU.mult, ALU.add).then_inc(*cv.mark("e1"))
                    own(cv, p, "e1")
                    dve.reciprocal(eq[:, :, :], eq[:, :, :]).then_inc(*cv.mark("e2"))
                    own(cv, p, "e2")
                    dve.scalar_tensor_tensor(eT[:, :, :], eT[:, :, :], 1.0, eq[:, :, :], ALU.add, ALU.mult).then_inc(*cv.mark("e3"))
                    own(cv, p, "e3")
                    dve.tensor_tensor(eT[:, :, :], eT[:, :, :], eT[:, :, :], ALU.mult).then_inc(*cv.mark("e4"))
                    own(cv, p, "e4")
                    dve.tensor_tensor(eT[:, :, :], eT[:, :, :], eT[:, :, :], ALU.mult).then_inc(*cv.mark("e5"))
                    own(cv, p, "e5")
                    dve.tensor_reduce(esum[:, :], eT[:, :, :], AX.X, ALU.add).then_inc(*cv.mark("esum"))
                    own(cv, p, "esum")
                    dve.reciprocal(emax[:, :], esum[:, :]).then_inc(*cv.mark("erec"))
                    own(cv, p, "erec")
                    dve.tensor_tensor(eTx, eT[:, :, :].unsqueeze(3).to_broadcast([T, 2, T, T]),
                                      emax[:, :].unsqueeze(2).to_broadcast([T, 2, T]).unsqueeze(3).to_broadcast([T, 2, T, T]), ALU.mult).then_inc(*cv.mark("ET"))
                if name == "Erep":
                    if isinstance(p, int) and p == 0:
                        dve.wait_ge(load["graph"], 96)
                        dve.tensor_scalar(vs_s[:, :, :], vs_s[:, :, :], 0.5, None, ALU.mult).then_inc(prep_dve, 1)
                    e = t[:, 0:128].rearrange("p (q s) -> p q s", q=4)
                    dve.tensor_scalar(ab[:, :, 32:48], e[:, :, 0:16], small_at("w3"), None, ALU.mult).then_inc(*cv.mark("EW"))
                    dve.tensor_tensor(ab[:, :, 0:16], small_at("w2").unsqueeze(1).to_broadcast([P, 4, T]), e[:, :, 16:17].to_broadcast([P, 4, T]), ALU.mult).then_inc(*cv.mark("WE"))
                if name in ("p2_0", "p2_1"):
                    b = int(name[3])
                    dve.tensor_tensor(th[:, b].rearrange("p c n -> p (c n)"), t[:, :], bs_s[:, :, :].rearrange("p c n -> p (c n)"), ALU.add).then_inc(*cv.mark(f"pb{b}"))
                if name in ("sp0", "sp1"):
                    b = int(name[2])
                    dve.tensor_reduce(smax[:, b, :], t[:, :].rearrange("p (c n) -> p c n", c=2), AX.X, ALU.max, negate=True).then_inc(*cv.mark(f"smax{b}"))
                if name in ("st0", "st1"):
                    b = int(name[2])
                    dve.wait_ge(conv_act.sem, conv_act.at(p, f"ex{b}1"))
                    dve.reciprocal(rinv[:, b, :], ssum[:, b, :]).then_inc(*cv.mark(f"rinv{b}"))
                    dve.wait_ge(filled(name).sem, filled(name).at(p, name))
                    for k in range(3):
                        dve.tensor_tensor(a_s[b][:, k].rearrange("p c n -> p (c n)"), t[:, :], cheb_s[:, k].rearrange("p c n -> p (c n)"), ALU.mult).then_inc(*cv.mark(f"A{b}{k}"))
                if name in ("tc0", "tc1"):
                    b = int(name[2])
                    for m in range(2):
                        dve.scalar_tensor_tensor(z[:, b, m, :], t[:, m * 256:(m + 1) * 256], rinv[:, b, m:m + 1], resb[:, b, m, :], ALU.mult, ALU.add).then_inc(*cv.mark(f"z{b}{m}"))
                if name == "z1":
                    for b in range(2):
                        dve.wait_ge(conv_act.sem, conv_act.at(p, f"relu{b}"))
                        dve.tensor_reduce(msum[:, b].rearrange("p (m o) -> p m o", m=2), by_time(z[:, b]), AX.X, ALU.add).then_inc(*cv.mark(f"sum{b}"))
                    own(cv, p, "sum1")
                    dve.tensor_scalar(msum[:, :, :], msum[:, :, :], 1.0 / T, None, ALU.mult).then_inc(*cv.mark("mean"))
                    own(cv, p, "mean")
                    for b in range(2):
                        zb = z[:, b].rearrange("p m (t o) -> p m t o", o=T)
                        dve.tensor_tensor(zb, zb, per_row(msum[:, b]), ALU.subtract).then_inc(*cv.mark(f"sub{b}"))
                    gm = small_at("gamma").unsqueeze(1).to_broadcast([P, 2, T]).unsqueeze(3).to_broadcast([P, 2, T, T])
                    for b in range(2):
                        own(cv, p, f"sub{b}")
                        dve.tensor_tensor(zg[:, b].rearrange("p m (t o) -> p m t o", o=T), z[:, b].rearrange("p m (t o) -> p m t o", o=T), gm,
                                          ALU.mult).then_inc(*cv.mark(f"zg{b}"))
                if name == "z2":
                    for b in range(2):
                        dve.wait_ge(conv_act.sem, conv_act.at(p, f"sq{b}"))
                        dve.tensor_reduce(vsum[:, b].rearrange("p (m o) -> p m o", m=2), by_time(zsq[:, b]), AX.X, ALU.add).then_inc(*cv.mark(f"vs{b}"))
                    own(cv, p, "vs1")
                    v, y, w = (t[:, :, :].rearrange("p b r -> p (b r)") for t in (vsum, vrstd, msum))
                    dve.tensor_scalar(v, v, 1.0 / T, 1e-5, ALU.mult, ALU.add).then_inc(*cv.mark("vv"))
                    own(cv, p, "vv")
                    dve.tensor_scalar(w.bitcast(I32), v.bitcast(I32), 1, None, ALU.arith_shift_right).then_inc(*cv.mark("half"))
                    own(cv, p, "half")
                    dve.tensor_scalar(y.bitcast(I32), w.bitcast(I32), -1, 0x5F3759DF, ALU.mult, ALU.add).then_inc(*cv.mark("guess"))
                    before = "guess"
                    for i in range(NEWTON):
                        own(cv, p, before)
                        dve.tensor_tensor(w, y, y, ALU.mult).then_inc(*cv.mark(f"yy{i}"))
                        own(cv, p, f"yy{i}")
                        dve.scalar_tensor_tensor(w, w, -0.5, v, ALU.mult, ALU.mult).then_inc(*cv.mark(f"yv{i}"))
                        own(cv, p, f"yv{i}")
                        dve.scalar_tensor_tensor(y, w, 1.5, y, ALU.add, ALU.mult).then_inc(*cv.mark(f"y{i}"))
                        before = f"y{i}"
                if name == "z3":
                    own(cv, p, f"y{NEWTON - 1}")
                    for b in range(2):
                        zb = zg[:, b].rearrange("p m (t o) -> p m t o", o=T)
                        dve.tensor_tensor(zb, zb, per_row(vrstd[:, b]), ALU.mult).then_inc(*cv.mark(f"n1{b}"))
                        own(cv, p, f"n1{b}")
                        dve.wait_ge(conv_pool.sem, conv_pool.at(p, f"xb{b}"))
                        x1v = x1[:, :, b, :].rearrange("p m (o t) -> p m o t", t=T)
                        dve.tensor_tensor(x1v, by_time(zg[:, b]), x1v, ALU.add).then_inc(*cv.mark(f"n3{b}"))
                if name in ("tok0", "tok1"):
                    layer_stats(p, at, t, int(name[3]))
                    if name == "tok1":
                        gather_stats(p, at)
                if name == "nrm":
                    apply_norm(p, at, attn_pool, ["tok0", "tok1"])
                if name in ("xl0", "xl1"):
                    c = int(name[2])
                    dve.wait_ge(attn_act.sem, attn_act.at(p, f"hi{c}"))
                    dve.tensor_tensor(xa_l[:, c, :], t[:, :], xa_h[:, c, :].bitcast(F32), ALU.subtract).then_inc(*at.mark(f"lo{c}"))
                if name in ("k0", "k1", "q0", "q1"):
                    c = int(name[1])
                    f = q_f if name[0] == "q" else k_f
                    dve.wait_ge(attn_act.sem, attn_act.at(p, "e" + name))
                    dve.tensor_scalar(e_s[:, c, :], e_s[:, c, :], 1.0, None, ALU.min).then_inc(*at.mark(f"{name[0]}min{c}"))
                    own(at, p, f"{name[0]}min{c}")
                    dve.scalar_tensor_tensor(f[:, c, :], t[:, :], 0.0, e_s[:, c, :], ALU.max, ALU.add).then_inc(*at.mark(name))
                if name == "k1":
                    for c in range(2):
                        own(at, p, f"k{c}")
                        for b in range(2):
                            k_b = k_f[:, c, b * L:(b + 1) * L]
                            dve.tensor_tensor_scan(zs[:, c, b * L:(b + 1) * L], k_b, k_b, 0.0, ALU.add, ALU.max).then_inc(*at.mark(f"scan{c}{b}"))
                if name in ("q0", "q1"):
                    c = int(name[1])
                    own(at, p, name)
                    dve.tensor_tensor(zs[:, c, :], zs[:, c, :], q_f[:, c, :], ALU.mult).then_inc(*at.mark(f"zq{c}"))
                if name == "kv":
                    dve.tensor_tensor(kvm[:, :].rearrange("p (q e) -> p q e", q=4), t[:, :].rearrange("p (q e) -> p q e", q=4),
                                      const_at("heads16").unsqueeze(1).to_broadcast([P, 4, P]), ALU.mult).then_inc(*at.mark("kvm"))
                if name == "dent":
                    dve.tensor_scalar(rd[:, :, :].rearrange("p q h -> p (q h)"), t[:, 0:64], 1e-5, None, ALU.add).then_inc(*at.mark("da"))
                    own(at, p, "da")
                    dve.reciprocal(rd[:, :, :], rd[:, :, :]).then_inc(*at.mark("dr"))
                if name in SCORES:
                    i = SCORES.index(name)
                    if i >= 3:
                        dve.wait_ge(pv_done.sem, pv_done.at(p, SCORES[i - 3]))
                    dve.wait_ge(filled(name).sem, filled(name).at(p, name))
                    dve.tensor_tensor(p_s[:, i % 3, :].rearrange("p (h l) -> p h l", h=4), t[:, :].rearrange("p (h l) -> p h l", h=4),
                                      const_at("causal").unsqueeze(1).to_broadcast([P, 4, P]), ALU.mult).then_inc(*at.mark(name))
                if name in ("at0", "at1"):
                    b = int(name[2])
                    dve.wait_ge(pv_done.sem, pv_done.at(p, SCORES[8 * b + 7]))
                    dve.wait_ge(attn_act.sem, attn_act.at(p, "rd1"))
                    dve.tensor_tensor(attn[:, :, b * L:(b + 1) * L], num[:, :].rearrange("p (c l) -> p c l", c=2),
                                      rd_s[:, :, b * L:(b + 1) * L], ALU.mult).then_inc(*at.mark(f"at{b}"))
                if name in ("wo0", "wo1"):
                    c = int(name[2])
                    if c == 0 and not (isinstance(p, int) and p == 0):
                        dve.wait_ge(x2_kept.sem, x2_kept.at(p - 1, "x2k"))
                    dve.scalar_tensor_tensor(x2[:, c, :], t[:, :], small_at("bo")[:, c:c + 1], x1[:, c].rearrange("p b l -> p (b l)"),
                                             ALU.add, ALU.add).then_inc(*at.mark(f"x2{c}"))
                if name in ("tk0", "tk1"):
                    layer_stats(p, rt, t, int(name[2]))
                    if name == "tk1":
                        gather_stats(p, rt)
                if name == "nrm2":
                    apply_norm(p, rt, route_pool, ["tk0", "tk1"])
                if name in ("xn0", "xn1"):
                    c = int(name[2])
                    dve.wait_ge(route_act.sem, route_act.at(p, f"hi{c}"))
                    dve.tensor_tensor(xf_l[:, c, :], t[:, :], xf_h[:, c, :].bitcast(F32), ALU.subtract).then_inc(*rt.mark(f"lo{c}"))
                if isinstance(p, int) and p == 0 and name in SPLIT_AT:
                    split(SPLIT_AT.index(name))

            def route(p, name):
                rt = route_dve
                if name == "r1":
                    route_groups(p, rt)
                if name == "r2":
                    route_choose_groups(p, rt)
                if name == "r3":
                    route_choose_experts(p, rt)
                if name == "r4":
                    route_weights(p, rt)

            def route_groups(p, rt):
                dve.wait_ge(route_act.sem, route_act.at(p, "eneg"))
                dve.tensor_scalar(sc[:, :, :], sc[:, :, :], 1.0, None, ALU.add).then_inc(*rt.mark("one"))
                own(rt, p, "one")
                dve.reciprocal(sc[:, :, :], sc[:, :, :]).then_inc(*rt.mark("sig"))
                own(rt, p, "sig")
                dve.tensor_tensor(scb[:, :, :], sc[:, :, :], small_at("corr").unsqueeze(1).to_broadcast([P, 4, EXPERTS]), ALU.add).then_inc(*rt.mark("sb"))
                own(rt, p, "sb")
                g = scb[:, :, :].rearrange("p q (g e) -> p (q g) e", e=4)
                dve.tensor_tensor(pairs[:, :, 0:3], g[:, :, 0:3], g[:, :, 1:4], ALU.add).then_inc(*rt.mark("p1"))
                dve.tensor_tensor(pairs[:, :, 3:5], g[:, :, 0:2], g[:, :, 2:4], ALU.add).then_inc(*rt.mark("p2"))
                dve.tensor_tensor(pairs[:, :, 5:6], g[:, :, 0:1], g[:, :, 3:4], ALU.add).then_inc(*rt.mark("p3"))
                own(rt, p, "p3")
                dve.tensor_reduce(gs[:, :, 0:4], pairs[:, :, :].rearrange("p (q g) s -> p q g s", q=4), AX.X, ALU.max).then_inc(*rt.mark("gs"))

            def route_choose_groups(p, rt):
                own(rt, p, "gs")
                carry(dve)
                for q in range(4):
                    dve.max(gtop[:, q, :], gs[:, q, :]).then_inc(*rt.mark(f"gx{q}"))
                own(rt, p, "gx3")
                dve.tensor_copy(gtake[:, :, 0:2], gtop[:, :, 0:2]).then_inc(*rt.mark("gt"))
                own(rt, p, "gt")
                carry(dve)
                for q in range(4):
                    dve.match_replace(gmark[:, q, :], gtake[:, q, :], gs[:, q, :], BIG).then_inc(*rt.mark(f"gr{q}"))
                own(rt, p, "gr3")
                dve.tensor_scalar(gneg[:, :, :], gmark[:, :, 0:4], BIG / 2, UNCHOSEN, ALU.is_lt, ALU.mult).then_inc(*rt.mark("gn"))
                own(rt, p, "gn")
                dve.tensor_tensor(es[:, :, 0:16].rearrange("p q (g e) -> p q g e", e=4), scb[:, :, :].rearrange("p q (g e) -> p q g e", e=4),
                                  gneg[:, :, :].unsqueeze(3).to_broadcast([P, 4, 4, 4]), ALU.add).then_inc(*rt.mark("es"))

            def route_choose_experts(p, rt):
                own(rt, p, "es")
                carry(dve)
                for q in range(4):
                    dve.max(etop[:, q, :], es[:, q, 0:16]).then_inc(*rt.mark(f"ex{q}"))
                own(rt, p, "ex3")
                dve.tensor_copy(etake[:, :, 0:4], etop[:, :, 0:4]).then_inc(*rt.mark("et"))
                own(rt, p, "et")
                carry(dve)
                for q in range(4):
                    dve.match_replace(emark[:, q, :], etake[:, q, :], es[:, q, :], BIG).then_inc(*rt.mark(f"er{q}"))

            def route_weights(p, rt):
                own(rt, p, "er3")
                dve.scalar_tensor_tensor(wsel[:, :, :], emark[:, :, 0:16], BIG / 2, sc[:, :, :], ALU.is_ge, ALU.mult).then_inc(*rt.mark("ws"))
                own(rt, p, "ws")
                dve.tensor_reduce(wsum[:, :], wsel[:, :, :], AX.X, ALU.add).then_inc(*rt.mark("wsum"))
                own(rt, p, "wsum")
                dve.tensor_scalar(wsum[:, :], wsum[:, :], 1e-20, None, ALU.add).then_inc(*rt.mark("weps"))
                own(rt, p, "weps")
                dve.reciprocal(wsum[:, :], wsum[:, :]).then_inc(*rt.mark("wrec"))
                own(rt, p, "wrec")
                dve.tensor_tensor(wsel[:, :, :], wsel[:, :, :], wsum[:, :].unsqueeze(2).to_broadcast([P, 4, EXPERTS]), ALU.mult).then_inc(*rt.mark("wn"))
                own(rt, p, "wn")
                dve.tensor_copy(whl[:, :, 0, :], wsel[:, :, :]).then_inc(*rt.mark("wh"))
                own(rt, p, "wh")
                dve.tensor_tensor(whl[:, :, 1, :], wsel[:, :, :], whl[:, :, 0, :].bitcast(F32), ALU.subtract).then_inc(*rt.mark("wl"))

            def ffn(p, kind, j):
                if kind == "h":
                    dve.wait_ge(ffn_pe.sem, ffn_pe.at(p, f"u{j}"))
                    dve.wait_ge(ffn_act.sem, ffn_act.at(p, f"si{j}"))
                    dve.wait_ge(ffn_dve.sem, ffn_dve.at(p, f"h{j}") - 1)
                    dve.tensor_tensor(hb, sl, u_ps[:, :], ALU.mult).then_inc(*ffn_dve.mark(f"h{j}"))
                if kind == "w" and j < ROUTED:
                    dve.wait_ge(ffn_pe.sem, ffn_pe.at(p, f"cm{j}"))
                    dve.wait_ge(ffn_dve.sem, ffn_dve.at(p, f"h{j}"))
                    dve.tensor_tensor(hb, hb, g_ps[:, :], ALU.mult).then_inc(*ffn_dve.mark(f"w{j}"))
                if kind == "w":
                    dve.wait_ge(ffn_act.sem, ffn_act.at(p, f"hi{j}"))
                    dve.tensor_tensor(hl[:, j % 2, :], hb, hh[:, j % 2, :].bitcast(F32), ALU.subtract).then_inc(*ffn_dve.mark(f"lo{j}"))
                if kind == "out":
                    dve.wait_ge(ffn_pe.sem, ffn_pe.at(p, f"dn{CHUNKS - 1}"))
                    dve.wait_ge(x2_kept.sem, x2_kept.at(p, "x2k"))
                    dve.wait_ge(out_stored, 32 * p + 32)
                    for m in range(2):
                        dve.tensor_tensor(y_out[:, m, :], d_ps[m][:, :], x2k[:, m, :], ALU.add).then_inc(*ffn_dve.mark(f"out{m}"))

            run((dve, front, route, ffn))

        @block.tensor
        def _(pe):
            pe.wait_ge(load["small"], 32)
            pe.wait_ge(prep_dve, 8)
            pe.wait_ge(prep_pool, 10)

            def split_products(t, cols, rhs_h, rhs_l, wh, wl):
                for k in range(2):
                    last = mm3(pe, t, wh[:, k, cols], wl[:, k, cols], rhs_h[:, k, :], rhs_l[:, k, :], k == 0, k == 1)
                return last

            def scores(p, n):
                b, lc, j = map(int, n[1:])
                wait_bank(pe, p, n)
                rows, cols = slice(32 * j, 32 * j + 32), slice(b * L + lc * P, b * L + lc * P + P)
                for c in range(2):
                    for odd in range(2):
                        last = pe.matmul(tile(n)[:, (2 * c + odd) * P:(2 * c + odd + 1) * P], k_f[rows, c, cols],
                                         (q_o if odd else q_e)[rows, c, cols], start=True, stop=True, tile_position=(32 * j, 0))
                last.then_inc(*filled(n).mark(n))

            def weigh(p, n):
                b, lc, j = map(int, n[1:])
                pe.wait_ge(attn_dve.sem, attn_dve.at(p, n))
                rows = slice(32 * j, 32 * j + 32)
                i = SCORES.index(n)
                for c in range(2):
                    for odd in range(2):
                        last = pe.matmul(num[rows, c * L + lc * P:c * L + lc * P + P], v_s[:, b, lc, 4 * c + j, 16 * odd:16 * odd + 32],
                                         p_s[:, i % 3, (2 * c + odd) * P:(2 * c + odd + 1) * P], start=(lc == 0 and c == 0 and odd == 0),
                                         stop=(odd == 1), skip_group_check=True, tile_position=(0, 32 * j))
                last.then_inc(*pv_done.mark(n))

            def front(p, name):
                t = tile(name) if name in TILES else None
                if name in TILES and name not in SCORES:
                    wait_bank(pe, p, name)
                if name == "gn":
                    pe.wait_ge(conv_dve.sem, conv_dve.at(p, "m2"))
                    pe.matmul(t[:, 0:8], const_at("mean8"), mv[:, :, :].rearrange("p q s -> p (q s)"), start=True, stop=True).then_inc(*filled(name).mark(name))
                if name in ("xT0", "xT1"):
                    b = int(name[2])
                    for c in range(2):
                        for m in range(2):
                            if c == 0:
                                pe.wait_ge(conv_dve.sem, conv_dve.at(p, f"xg{2 * b + m}"))
                            last = pe.transpose(t[:, c * N + m * P:c * N + (m + 1) * P], xg[:, b, m, c * P:(c + 1) * P], ident)
                    last.then_inc(*filled(name).mark(name))
                if name == "M":
                    pe.wait_ge(conv_dve.sem, conv_dve.at(p, "xg3"))
                    for b in range(2):
                        for m in range(2):
                            last = pe.matmul(t[:, b * 256:(b + 1) * 256], small_at("u2")[:, m * P:(m + 1) * P], xg[:, b, m, :], start=(m == 0), stop=(m == 1))
                    last.then_inc(*filled(name).mark(name))
                if name[0] == "y":
                    b, m, c = map(int, name[1:])
                    if isinstance(p, int) and p == 0:
                        pe.wait_ge(load["blocks"], 256)
                    pe.matmul(t[:, :], xT[:, b, c, m * P:(m + 1) * P], theta_s[:, :, :, :].rearrange("p k t o -> p (k t o)"), start=True, stop=True).then_inc(*filled(name).mark(name))
                if name == "prod":
                    pe.wait_ge(conv_dve.sem, conv_dve.at(p, "M"))
                    pe.wait_ge(conv_dve.sem, conv_dve.at(p, "Lm"))
                    for b in range(2):
                        for c in range(2):
                            last = pe.matmul(t[0:T, b * T:(b + 1) * T], m_s[:, b * T:(b + 1) * T], lm[:, b, c, :], start=(c == 0), stop=(c == 1))
                    last.then_inc(*filled(name).mark(name))
                if name == "Epre":
                    pe.wait_ge(conv_act.sem, conv_act.at(p, "thE"))
                    pe.matmul(t[0:4 * T, 0:32], ve_h[:, :, :].rearrange("p r s -> p (r s)"), te[:, :, :].rearrange("p b s -> p (b s)"), start=True, stop=True).then_inc(*filled(name).mark(name))
                if name == "Erep":
                    pe.wait_ge(conv_dve.sem, conv_dve.at(p, "ET"))
                    for b in range(2):
                        for c in range(2):
                            o = (2 * b + c) * 32
                            last = pe.matmul(t[:, o:o + 17], eTx[:, b, 8 * c:8 * c + 8].rearrange("p j f -> p (j f)"), iw1[:, 0:17], start=True, stop=True)
                    last.then_inc(*filled(name).mark(name))
                if name == "lr":
                    pe.wait_ge(conv_dve.sem, conv_dve.at(p, "WE"))
                    for b in range(2):
                        for c in range(2):
                            last = pe.matmul(t[0:64, b * N:(b + 1) * N], ab[:, 2 * b + c, :], xT[:, b, c, :], start=(c == 0), stop=(c == 1))
                    last.then_inc(*filled(name).mark(name))
                if name in ("p2_0", "p2_1"):
                    b = int(name[3])
                    pe.wait_ge(conv_act.sem, conv_act.at(p, "r2"))
                    for m in range(2):
                        last = pe.matmul(t[:, m * N:(m + 1) * N], r2[:, b * N + m * P:b * N + (m + 1) * P], l2[:, b * N:(b + 1) * N], start=True, stop=True)
                    last.then_inc(*filled(name).mark(name))
                if name in ("sp0", "sp1"):
                    b = int(name[2])
                    if isinstance(p, int) and p == 0:
                        pe.wait_ge(prep_dve, 9)
                    pe.wait_ge(conv_act.sem, conv_act.at(p, f"th{b}"))
                    for kc in range(2):
                        for jc in range(2):
                            last = pe.matmul(t[:, kc * N:(kc + 1) * N], vs_s[:, jc, kc * P:(kc + 1) * P], th[:, b, jc, :], start=(jc == 0), stop=(jc == 1))
                    last.then_inc(*filled(name).mark(name))
                if name in ("st0", "st1"):
                    b = int(name[2])
                    pe.wait_ge(conv_act.sem, conv_act.at(p, f"ex{b}1"))
                    for kc in range(2):
                        for ic in range(2):
                            last = pe.transpose(t[:, ic * N + kc * P:ic * N + (kc + 1) * P], sT[:, b, kc, ic * P:(ic + 1) * P], ident)
                    last.then_inc(*filled(name).mark(name))
                if name in ("o0", "o1"):
                    b = int(name[1])
                    pe.wait_ge(conv_dve.sem, conv_dve.at(p, f"A{b}2"))
                    pe.wait_ge(conv_act.sem, conv_act.at(p, f"y{b}11"))
                    for c in range(2):
                        for k in range(3):
                            for m in range(2):
                                last = pe.matmul(t[:, c * N:(c + 1) * N], y_s[:, b, m, c, k * P:(k + 1) * P], a_s[b][:, k, m, :],
                                                 start=(k == 0 and m == 0), stop=(k == 2 and m == 1))
                    last.then_inc(*filled(name).mark(name))
                if name in ("tc0", "tc1"):
                    b = int(name[2])
                    pe.wait_ge(conv_act.sem, conv_act.at(p, f"sg{b}"))
                    band = tconv_s[:, :, :].rearrange("p r o -> p (r o)")
                    for m in range(2):
                        pe.matmul(t[:, m * 256:m * 256 + 144], sg[:, b, 0, m * P:(m + 1) * P], band[:, 16:160], start=True, stop=False, skip_group_check=True)
                        last = pe.matmul(t[:, m * 256 + 112:m * 256 + 256], sg[:, b, 1, m * P:(m + 1) * P], band[:, 0:144], start=False, stop=True, skip_group_check=True)
                    last.then_inc(*filled(name).mark(name))
                if name in ("tok0", "tok1", "tk0", "tk1"):
                    b = int(name[-1])
                    if name[1] == "o":
                        pe.wait_ge(conv_dve.sem, conv_dve.at(p, f"n3{b}"))
                    else:
                        pe.wait_ge(attn_dve.sem, attn_dve.at(p, "x21"))
                    for lc in range(2):
                        for c in range(2):
                            src = x1[:, c, b, lc * P:(lc + 1) * P] if name[1] == "o" else x2[:, c, b * L + lc * P:b * L + (lc + 1) * P]
                            last = pe.transpose(t[:, lc * N + c * P:lc * N + (c + 1) * P], src, ident)
                    last.then_inc(*filled(name).mark(name))
                if name in ("xl0", "xl1", "xn0", "xn1"):
                    c = int(name[2])
                    sig = attn_dve if name[1] == "l" else route_dve
                    pe.wait_ge(sig.sem, sig.at(p, "nm3"))
                    for q in range(4):
                        last = pe.transpose(t[:, q * P:(q + 1) * P], xt[:, q // 2, q % 2, c * P:(c + 1) * P], ident)
                    last.then_inc(*filled(name).mark(name))
                if name in ("q0", "q1", "k0", "k1"):
                    c = int(name[1])
                    pe.wait_ge(attn_dve.sem, attn_dve.at(p, "lo1"))
                    o = c * P + (N if name[0] == "k" else 0)
                    split_products(t[:, :], slice(o, o + P), xa_h, xa_l, wqkv_h, wqkv_l).then_inc(*filled(name).mark(name))
                if name in ("v0", "v1"):
                    b = int(name[1])
                    for lc in range(2):
                        cols = slice(b * L + lc * P, b * L + (lc + 1) * P)
                        for k in range(2):
                            last = mm3(pe, t[:, lc * N:(lc + 1) * N], xa_h[:, k, cols], xa_l[:, k, cols], wqkv_h[:, k, 2 * N:], wqkv_l[:, k, 2 * N:], k == 0, k == 1)
                    last.then_inc(*filled(name).mark(name))
                if name == "kt":
                    pe.wait_ge(attn_dve.sem, attn_dve.at(p, "k1"))
                    for b in range(2):
                        for c in range(2):
                            last = pe.transpose(t[:, (2 * b + c) * P:(2 * b + c + 1) * P], k_f[:, c, b * L:b * L + P], ident)
                    last.then_inc(*filled(name).mark(name))
                if name == "kv":
                    pe.wait_ge(attn_act.sem, attn_act.at(p, "kt"))
                    for b in range(2):
                        for c in range(2):
                            q = 2 * b + c
                            for odd in range(2):
                                last = pe.matmul(t[:, q * P:(q + 1) * P], ktok[:, q * P:(q + 1) * P], v_s[:, b, 0, 4 * c:4 * c + 4, 16 * odd:16 * odd + 32],
                                                 start=(odd == 0), stop=(odd == 1))
                    last.then_inc(*filled(name).mark(name))
                if name == "dent":
                    pe.wait_ge(attn_dve.sem, attn_dve.at(p, "zq1"))
                    for q in range(4):
                        for c in range(2):
                            last = pe.matmul(t[:, q * 16 + 8 * c:q * 16 + 8 * c + 8], zs[:, c, q * P:(q + 1) * P], const_at("head"), start=True, stop=True)
                    last.then_inc(*filled(name).mark(name))
                if name in ("rd0", "rd1"):
                    c = int(name[2])
                    pe.wait_ge(attn_act.sem, attn_act.at(p, "rdx"))
                    for q in range(4):
                        last = pe.matmul(t[:, q * P:(q + 1) * P], rdx[:, q, 8 * c:8 * c + 8].rearrange("p h e -> p (h e)"), ident, start=True, stop=True)
                    last.then_inc(*filled(name).mark(name))
                if name in ("P0", "P1"):
                    b = int(name[1])
                    pe.wait_ge(attn_act.sem, attn_act.at(p, "rd1"))
                    pe.wait_ge(attn_dve.sem, attn_dve.at(p, "kvm" if b == 0 else "at0"))
                    scores(p, SCORES[8 * b])
                    scores(p, SCORES[8 * b + 1])
                if name in SCORES:
                    i = SCORES.index(name)
                    b = i // 8
                    if i % 8 + 2 < 8:
                        scores(p, SCORES[i + 2])
                    if i % 8 == 4:
                        for c in range(2):
                            pe.matmul(num[:, c * L + P:(c + 1) * L], kvm[:, (2 * b + c) * P:(2 * b + c + 1) * P], q_f[:, c, b * L + P:(b + 1) * L],
                                      start=False, stop=False, skip_group_check=True)
                    weigh(p, name)
                if name in ("wo0", "wo1"):
                    c = int(name[2])
                    pe.wait_ge(attn_dve.sem, attn_dve.at(p, "at1"))
                    for k in range(2):
                        last = pe.matmul(t[:, :], wo_s[:, k, c * P:(c + 1) * P], attn[:, k, :], start=(k == 0), stop=(k == 1))
                    last.then_inc(*filled(name).mark(name))

            def route(p, name):
                t = num
                if name == "lg":
                    pe.wait_ge(route_dve.sem, route_dve.at(p, "lo1"))
                    split_products(t[:, :], slice(0, P), xf_h, xf_l, router_h, router_l).then_inc(*route_pe.mark(name))
                if name == "rt":
                    pe.wait_ge(route_act.sem, route_act.at(p, "lg"))
                    for q in range(4):
                        last = pe.matmul(t[:, q * 16:(q + 1) * 16], lgT[:, q * P:(q + 1) * P], ident[0:16, 0:16], start=True, stop=True)
                    last.then_inc(*route_pe.mark(name))
                if name == "cb":
                    pe.wait_ge(route_dve.sem, route_dve.at(p, "wl"))
                    for q in range(4):
                        last = pe.transpose(t[0:32, q * P:(q + 1) * P], whl[:, q].rearrange("p s e -> p (s e)").bitcast(F32), ident)
                    last.then_inc(*route_pe.mark(name))

            def ffn(p, kind, j):
                if kind == "gu":
                    cols = slice(j * P, (j + 1) * P)
                    if j == 0:
                        pe.wait_ge(route_dve.sem, route_dve.at(p, "lo1"))
                        if not isinstance(p, int):
                            pe.wait_ge(piece_low, len(PIECES) - 1)
                            pe.wait_ge(piece_high, len(PIECES))
                    if j:
                        pe.wait_ge(ffn_dve.sem, ffn_dve.at(p, f"w{j - 1}" if j - 1 < ROUTED else f"h{j - 1}"))
                    split_products(g_ps[:, :], cols, xf_h, xf_l, gate_h, gate_l).then_inc(*ffn_pe.mark(f"g{j}"))
                    split_products(u_ps[:, :], cols, xf_h, xf_l, up_h, up_l).then_inc(*ffn_pe.mark(f"u{j}"))
                if kind == "h" and j < ROUTED:
                    pe.wait_ge(route_act.sem, route_act.at(p, "cb"))
                    pe.wait_ge(ffn_act.sem, ffn_act.at(p, f"si{j}"))
                    pe.matmul(g_ps[:, :], spread[:, j, :], comb[:, :], start=True, stop=True).then_inc(*ffn_pe.mark(f"cm{j}"))
                if kind == "dn":
                    pe.wait_ge(ffn_dve.sem, ffn_dve.at(p, f"lo{j}"))
                    for m in range(2):
                        last = mm3(pe, d_ps[m][:, :], down_h[:, j, m * P:(m + 1) * P], down_l[:, j, m * P:(m + 1) * P],
                                   hh[:, j % 2, :], hl[:, j % 2, :], j == 0, j == CHUNKS - 1)
                    last.then_inc(*ffn_pe.mark(f"dn{j}"))

            run((pe, front, route, ffn))


def kernel(**inputs):
    import numpy as _np
    import concourse.bacc as _bacc
    from concourse import mybir as _mybir
    from concourse.bass_utils import run_bass_kernel_spmd as _run

    a = {k: _np.ascontiguousarray(v) for k, v in inputs.items()}
    f32 = _np.float32

    def rows(v):
        return _np.broadcast_to(v, (P, v.shape[-1]))

    def by_tf(v):
        return _np.concatenate([v] * 8, axis=0)

    def short(v):
        full = _np.zeros((P, v.shape[1]), f32)
        full[:v.shape[0]] = v
        return full

    u2 = a["L0_conv_U2"].T.reshape(2, P, 1, T)
    u2 = _np.broadcast_to(u2, (2, P, 8, T)).transpose(1, 0, 2, 3).reshape(P, 256)
    small = _np.concatenate([
        rows(a["L0_conv_U1"][None]), u2, rows(a["L0_conv_U3"][None]), by_tf(a["L0_conv_W3"][:, None]),
        by_tf(a["L0_conv_W2"]), short(a["L0_conv_W1"][:, None]), short(a["L0_conv_V_e"].T), short(a["L0_conv_b_e"][0].T),
        rows(a["L0_conv_tb"][None]), rows(a["L0_conv_rb"][None]), rows(a["L0_conv_gamma"][None]), rows(a["L0_conv_beta"][None]),
        a["L1_attn_bo"].reshape(2, P).T, a["L1_ffn_router_w"].T.reshape(2, P, 16).transpose(1, 0, 2).reshape(P, 32),
        rows(a["L1_ffn_correction_bias"][None])], axis=1)

    p = _np.arange(P)
    c = {
        "ident": p[:, None] == p[None], "mean8": (p[:, None] // 8 == p[None] // 8) / 8.0,
        "heads16": p[:, None] // 16 == p[None] // 16, "causal": p[:, None] <= p[None],
        "even": (p[:, None] // 16) % 2 == 0, "odd": (p[:, None] // 16) % 2 == 1,
        "halves": _np.concatenate([p[:, None] // 16 + 8 * h == _np.arange(16)[None] for h in range(2)], axis=1),
        "head": p[:, None] // 16 == _np.arange(8)[None],
    }
    consts = _np.concatenate([c[n].astype(f32) for n in CONST], axis=1)
    spread = (_np.arange(32)[:, None] % 16 == _np.arange(1024)[None] // HIDDEN).astype(f32).reshape(32, ROUTED, P)
    theta = _np.concatenate([a["L0_conv_Theta"], a["L0_conv_rw"].T[None]], axis=0).transpose(1, 0, 2)
    tconv = a["L0_conv_tw"][:, :, 0, ::-1].transpose(1, 2, 0)
    given = {
        "x": a["x"], "small": small, "consts": consts, "spread_rows": spread, "cheb": a["L0_conv_cheb"], "theta": theta, "tconv": tconv,
        "vsT": a["L0_conv_V_s"].T, "bsT": a["L0_conv_b_s"][0].T,
        "wqkvT": _np.concatenate([a["L1_attn_Wq"].T, a["L1_attn_Wk"].T, a["L1_attn_Wv"].T], axis=1), "woT": a["L1_attn_Wo"].T,
        "gateT": _np.concatenate([a["L1_ffn_gate_w"].transpose(1, 0, 2).reshape(256, -1), a["L1_ffn_shared_gate_w"].T], axis=1),
        "upT": _np.concatenate([a["L1_ffn_up_w"].transpose(1, 0, 2).reshape(256, -1), a["L1_ffn_shared_up_w"].T], axis=1),
        "down": _np.concatenate([a["L1_ffn_down_w"].reshape(-1, 256), a["L1_ffn_shared_down_w"].T], axis=0),
    }
    nc = _bacc.Bacc("TRN2", target_bir_lowering=False, num_devices=1, dynamic_dma_scratch_size=4096)
    arrays, args = {}, {}
    for name, v in given.items():
        v = _np.ascontiguousarray(v)
        arrays[f"in_{name}"] = v
        args[name] = nc.dram_tensor(f"in_{name}", v.shape, _mybir.dt.from_np(v.dtype), kind="ExternalInput").ap()
    args["out"] = nc.dram_tensor("out_x", a["x"].shape, F32, kind="ExternalOutput").ap()
    graph_attention_moe(nc, **args)
    r = _run(nc, [arrays], core_ids=[0])
    return r.results[0]["out_x"]
```
